# Optimizing a Trainium2 kernel written in Bass

```python
import numpy as np
import jax
import jax.numpy as jnp

def _softmax(x, axis=-1):
    return jax.nn.softmax(x, axis=axis)

def _gelu(x):
    return jax.nn.gelu(x, approximate=True)

def _silu(x):
    return jax.nn.silu(x)

def _sigmoid(x):
    return jax.nn.sigmoid(x)

def _layernorm(x, axis=-1, eps=1e-05):
    m = jnp.mean(x, axis=axis, keepdims=True)
    v = jnp.var(x, axis=axis, keepdims=True)
    return (x - m) / jnp.sqrt(v + eps)

def _scatter_add(tgt, idx, src, axis=0):
    return tgt.at[idx].add(src)

def _segment_sum(src, seg, n):
    return jax.ops.segment_sum(src, seg, n)
kernel_name = 'mk_dlrm_tower_d1_rec_r8_0f9653'

def setup_inputs(seed: int=0):
    np.random.seed(seed)
    _w = jnp.asarray

    def _rec_inputs():
        import jax
        import jax.numpy as jnp
        _tk = jax.random.key(seed)
        dense_ctx = jax.random.normal(jax.random.fold_in(_tk, 190), (2048, 16), jnp.float32)
        ids = jnp.stack([jax.random.randint(jax.random.fold_in(_tk, 200 + f), (2048,), 0, v, jnp.int32) for f, v in enumerate([125000, 12500, 1000, 12500, 12500, 125000, 125000, 1250, 1000, 125000, 1250, 12500, 12500, 125000, 1000, 12500, 1000, 125000, 1250, 12500, 1250, 12500, 1000, 1250, 1000, 12500, 125000, 1250, 1000, 12500, 125000, 125000, 1000, 1250, 1250, 12500, 1000, 12500, 125000])], axis=1)
        tbl_0 = 0.05 * jax.random.normal(jax.random.fold_in(_tk, 500 + 0), (125000, 16), jnp.float32)
        tbl_1 = 0.05 * jax.random.normal(jax.random.fold_in(_tk, 500 + 1), (12500, 16), jnp.float32)
        tbl_2 = 0.05 * jax.random.normal(jax.random.fold_in(_tk, 500 + 2), (1000, 16), jnp.float32)
        tbl_3 = 0.05 * jax.random.normal(jax.random.fold_in(_tk, 500 + 3), (12500, 16), jnp.float32)
        tbl_4 = 0.05 * jax.random.normal(jax.random.fold_in(_tk, 500 + 4), (12500, 16), jnp.float32)
        tbl_5 = 0.05 * jax.random.normal(jax.random.fold_in(_tk, 500 + 5), (125000, 16), jnp.float32)
        tbl_6 = 0.05 * jax.random.normal(jax.random.fold_in(_tk, 500 + 6), (125000, 16), jnp.float32)
        tbl_7 = 0.05 * jax.random.normal(jax.random.fold_in(_tk, 500 + 7), (1250, 16), jnp.float32)
        tbl_8 = 0.05 * jax.random.normal(jax.random.fold_in(_tk, 500 + 8), (1000, 16), jnp.float32)
        tbl_9 = 0.05 * jax.random.normal(jax.random.fold_in(_tk, 500 + 9), (125000, 16), jnp.float32)
        tbl_10 = 0.05 * jax.random.normal(jax.random.fold_in(_tk, 500 + 10), (1250, 16), jnp.float32)
        tbl_11 = 0.05 * jax.random.normal(jax.random.fold_in(_tk, 500 + 11), (12500, 16), jnp.float32)
        tbl_12 = 0.05 * jax.random.normal(jax.random.fold_in(_tk, 500 + 12), (12500, 16), jnp.float32)
        tbl_13 = 0.05 * jax.random.normal(jax.random.fold_in(_tk, 500 + 13), (125000, 16), jnp.float32)
        tbl_14 = 0.05 * jax.random.normal(jax.random.fold_in(_tk, 500 + 14), (1000, 16), jnp.float32)
        tbl_15 = 0.05 * jax.random.normal(jax.random.fold_in(_tk, 500 + 15), (12500, 16), jnp.float32)
        tbl_16 = 0.05 * jax.random.normal(jax.random.fold_in(_tk, 500 + 16), (1000, 16), jnp.float32)
        tbl_17 = 0.05 * jax.random.normal(jax.random.fold_in(_tk, 500 + 17), (125000, 16), jnp.float32)
        tbl_18 = 0.05 * jax.random.normal(jax.random.fold_in(_tk, 500 + 18), (1250, 16), jnp.float32)
        tbl_19 = 0.05 * jax.random.normal(jax.random.fold_in(_tk, 500 + 19), (12500, 16), jnp.float32)
        tbl_20 = 0.05 * jax.random.normal(jax.random.fold_in(_tk, 500 + 20), (1250, 16), jnp.float32)
        tbl_21 = 0.05 * jax.random.normal(jax.random.fold_in(_tk, 500 + 21), (12500, 16), jnp.float32)
        tbl_22 = 0.05 * jax.random.normal(jax.random.fold_in(_tk, 500 + 22), (1000, 16), jnp.float32)
        tbl_23 = 0.05 * jax.random.normal(jax.random.fold_in(_tk, 500 + 23), (1250, 16), jnp.float32)
        tbl_24 = 0.05 * jax.random.normal(jax.random.fold_in(_tk, 500 + 24), (1000, 16), jnp.float32)
        tbl_25 = 0.05 * jax.random.normal(jax.random.fold_in(_tk, 500 + 25), (12500, 16), jnp.float32)
        tbl_26 = 0.05 * jax.random.normal(jax.random.fold_in(_tk, 500 + 26), (125000, 16), jnp.float32)
        tbl_27 = 0.05 * jax.random.normal(jax.random.fold_in(_tk, 500 + 27), (1250, 16), jnp.float32)
        tbl_28 = 0.05 * jax.random.normal(jax.random.fold_in(_tk, 500 + 28), (1000, 16), jnp.float32)
        tbl_29 = 0.05 * jax.random.normal(jax.random.fold_in(_tk, 500 + 29), (12500, 16), jnp.float32)
        tbl_30 = 0.05 * jax.random.normal(jax.random.fold_in(_tk, 500 + 30), (125000, 16), jnp.float32)
        tbl_31 = 0.05 * jax.random.normal(jax.random.fold_in(_tk, 500 + 31), (125000, 16), jnp.float32)
        tbl_32 = 0.05 * jax.random.normal(jax.random.fold_in(_tk, 500 + 32), (1000, 16), jnp.float32)
        tbl_33 = 0.05 * jax.random.normal(jax.random.fold_in(_tk, 500 + 33), (1250, 16), jnp.float32)
        tbl_34 = 0.05 * jax.random.normal(jax.random.fold_in(_tk, 500 + 34), (1250, 16), jnp.float32)
        tbl_35 = 0.05 * jax.random.normal(jax.random.fold_in(_tk, 500 + 35), (12500, 16), jnp.float32)
        tbl_36 = 0.05 * jax.random.normal(jax.random.fold_in(_tk, 500 + 36), (1000, 16), jnp.float32)
        tbl_37 = 0.05 * jax.random.normal(jax.random.fold_in(_tk, 500 + 37), (12500, 16), jnp.float32)
        tbl_38 = 0.05 * jax.random.normal(jax.random.fold_in(_tk, 500 + 38), (125000, 16), jnp.float32)
        _rk = jax.random.fold_in(_tk, 7)
        W_top1 = 0.0606339 * jax.random.normal(jax.random.fold_in(_tk, 801), (272, 512), jnp.float32)
        W_top2 = 0.0441942 * jax.random.normal(jax.random.fold_in(_tk, 802), (512, 256), jnp.float32)
        W_top3 = 0.0625 * jax.random.normal(jax.random.fold_in(_tk, 803), (256, 1), jnp.float32)
        b_top1 = jnp.zeros((512,), jnp.float32)
        b_top2 = jnp.zeros((256,), jnp.float32)
        return (dense_ctx, ids, tbl_0, tbl_1, tbl_2, tbl_3, tbl_4, tbl_5, tbl_6, tbl_7, tbl_8, tbl_9, tbl_10, tbl_11, tbl_12, tbl_13, tbl_14, tbl_15, tbl_16, tbl_17, tbl_18, tbl_19, tbl_20, tbl_21, tbl_22, tbl_23, tbl_24, tbl_25, tbl_26, tbl_27, tbl_28, tbl_29, tbl_30, tbl_31, tbl_32, tbl_33, tbl_34, tbl_35, tbl_36, tbl_37, tbl_38, W_top1, b_top1, W_top2, b_top2, W_top3)
    dense_ctx, ids, tbl_0, tbl_1, tbl_2, tbl_3, tbl_4, tbl_5, tbl_6, tbl_7, tbl_8, tbl_9, tbl_10, tbl_11, tbl_12, tbl_13, tbl_14, tbl_15, tbl_16, tbl_17, tbl_18, tbl_19, tbl_20, tbl_21, tbl_22, tbl_23, tbl_24, tbl_25, tbl_26, tbl_27, tbl_28, tbl_29, tbl_30, tbl_31, tbl_32, tbl_33, tbl_34, tbl_35, tbl_36, tbl_37, tbl_38, W_top1, b_top1, W_top2, b_top2, W_top3 = _rec_inputs()

    def _L0_rec_setup():
        import jax, jax.numpy as jnp
        import numpy as np
        B, M, D = (1024, 39, 16)
        S1, S2 = (128, 128)

        def _cin_layer(x0, xk, W, b):
            out = jnp.einsum('bhd,bmd,shm->bsd', xk, x0, W) + b[None, :, None]
            return jax.nn.relu(out)
        key = jax.random.key(seed)
        k0, k1, k2 = jax.random.split(key, 3)
        x0 = jax.random.normal(k0, (B, M, D), dtype=jnp.float32)
        W1 = jax.random.normal(k1, (S1, M, M), dtype=jnp.float32) * 0.05
        b1 = jnp.zeros((S1,), dtype=jnp.float32)
        W2 = jax.random.normal(k2, (S2, S1, M), dtype=jnp.float32) * 0.05
        b2 = jnp.zeros((S2,), dtype=jnp.float32)
        return {'x0': x0, 'W1': W1, 'b1': b1, 'W2': W2, 'b2': b2}
    _L0_rec_all = _L0_rec_setup()
    _L0_rec_in = {k: v for k, v in _L0_rec_all.items() if k in ('W1', 'b1', 'W2', 'b2')}
    del _L0_rec_all
    return {'dense_ctx': dense_ctx, 'ids': ids, 'tbl_0': tbl_0, 'tbl_1': tbl_1, 'tbl_2': tbl_2, 'tbl_3': tbl_3, 'tbl_4': tbl_4, 'tbl_5': tbl_5, 'tbl_6': tbl_6, 'tbl_7': tbl_7, 'tbl_8': tbl_8, 'tbl_9': tbl_9, 'tbl_10': tbl_10, 'tbl_11': tbl_11, 'tbl_12': tbl_12, 'tbl_13': tbl_13, 'tbl_14': tbl_14, 'tbl_15': tbl_15, 'tbl_16': tbl_16, 'tbl_17': tbl_17, 'tbl_18': tbl_18, 'tbl_19': tbl_19, 'tbl_20': tbl_20, 'tbl_21': tbl_21, 'tbl_22': tbl_22, 'tbl_23': tbl_23, 'tbl_24': tbl_24, 'tbl_25': tbl_25, 'tbl_26': tbl_26, 'tbl_27': tbl_27, 'tbl_28': tbl_28, 'tbl_29': tbl_29, 'tbl_30': tbl_30, 'tbl_31': tbl_31, 'tbl_32': tbl_32, 'tbl_33': tbl_33, 'tbl_34': tbl_34, 'tbl_35': tbl_35, 'tbl_36': tbl_36, 'tbl_37': tbl_37, 'tbl_38': tbl_38, 'W_top1': W_top1, 'b_top1': b_top1, 'W_top2': W_top2, 'b_top2': b_top2, 'W_top3': W_top3, 'L0_rec_W1': _L0_rec_in['W1'], 'L0_rec_b1': _L0_rec_in['b1'], 'L0_rec_W2': _L0_rec_in['W2'], 'L0_rec_b2': _L0_rec_in['b2']}

def reference(dense_ctx, ids, tbl_0, tbl_1, tbl_2, tbl_3, tbl_4, tbl_5, tbl_6, tbl_7, tbl_8, tbl_9, tbl_10, tbl_11, tbl_12, tbl_13, tbl_14, tbl_15, tbl_16, tbl_17, tbl_18, tbl_19, tbl_20, tbl_21, tbl_22, tbl_23, tbl_24, tbl_25, tbl_26, tbl_27, tbl_28, tbl_29, tbl_30, tbl_31, tbl_32, tbl_33, tbl_34, tbl_35, tbl_36, tbl_37, tbl_38, W_top1, b_top1, W_top2, b_top2, W_top3, L0_rec_W1, L0_rec_b1, L0_rec_W2, L0_rec_b2):
    import jax
    import jax.numpy as jnp

    def _L0_rec_ref(x0, W1, b1, W2, b2):
        import jax, jax.numpy as jnp
        import numpy as np
        B, M, D = (1024, 39, 16)
        S1, S2 = (128, 128)

        def _cin_layer(x0, xk, W, b):
            out = jnp.einsum('bhd,bmd,shm->bsd', xk, x0, W) + b[None, :, None]
            return jax.nn.relu(out)
        x1 = _cin_layer(x0, x0, W1, b1)
        x2 = _cin_layer(x0, x1, W2, b2)
        p1 = x1.sum(axis=-1)
        p2 = x2.sum(axis=-1)
        return jnp.concatenate([p1, p2], axis=-1)
    e = jnp.stack([tbl_0[ids[:, 0]], tbl_1[ids[:, 1]], tbl_2[ids[:, 2]], tbl_3[ids[:, 3]], tbl_4[ids[:, 4]], tbl_5[ids[:, 5]], tbl_6[ids[:, 6]], tbl_7[ids[:, 7]], tbl_8[ids[:, 8]], tbl_9[ids[:, 9]], tbl_10[ids[:, 10]], tbl_11[ids[:, 11]], tbl_12[ids[:, 12]], tbl_13[ids[:, 13]], tbl_14[ids[:, 14]], tbl_15[ids[:, 15]], tbl_16[ids[:, 16]], tbl_17[ids[:, 17]], tbl_18[ids[:, 18]], tbl_19[ids[:, 19]], tbl_20[ids[:, 20]], tbl_21[ids[:, 21]], tbl_22[ids[:, 22]], tbl_23[ids[:, 23]], tbl_24[ids[:, 24]], tbl_25[ids[:, 25]], tbl_26[ids[:, 26]], tbl_27[ids[:, 27]], tbl_28[ids[:, 28]], tbl_29[ids[:, 29]], tbl_30[ids[:, 30]], tbl_31[ids[:, 31]], tbl_32[ids[:, 32]], tbl_33[ids[:, 33]], tbl_34[ids[:, 34]], tbl_35[ids[:, 35]], tbl_36[ids[:, 36]], tbl_37[ids[:, 37]], tbl_38[ids[:, 38]]], axis=1)
    z = _L0_rec_ref(e, L0_rec_W1, L0_rec_b1, L0_rec_W2, L0_rec_b2)
    z = z.reshape(z.shape[0], -1)
    h = jnp.concatenate([z, dense_ctx], axis=1)
    h = jnp.maximum(h @ W_top1 + b_top1, 0.0)
    h = jnp.maximum(h @ W_top2 + b_top2, 0.0)
    y = h @ W_top3
    return y

_drawn_inputs = setup_inputs


def setup_inputs(seed=0):
    import zlib

    import numpy as np

    out = dict(_drawn_inputs(seed))
    spreads = {'b_top1': (0.0, 0.1),
     'b_top2': (0.0, 0.1),
     'L0_rec_b1': (0.0, 0.1),
     'L0_rec_b2': (0.0, 0.1)}
    factors = {'tbl_0': 4.692,
     'tbl_1': 4.412,
     'tbl_2': 7.655,
     'tbl_3': 6.196,
     'tbl_4': 6.465,
     'tbl_5': 7.359,
     'tbl_6': 5.559,
     'tbl_7': 4.538,
     'tbl_8': 8.0,
     'tbl_9': 7.156,
     'tbl_10': 6.356,
     'tbl_11': 5.758,
     'tbl_12': 5.396,
     'tbl_14': 8.0,
     'tbl_15': 6.365,
     'tbl_16': 7.344,
     'tbl_17': 4.612,
     'tbl_18': 5.422,
     'tbl_19': 4.478,
     'tbl_20': 8.0,
     'tbl_21': 3.338,
     'tbl_22': 8.0,
     'tbl_23': 7.276,
     'tbl_24': 7.732,
     'tbl_25': 4.987,
     'tbl_26': 4.492,
     'tbl_27': 6.732,
     'tbl_28': 7.922,
     'tbl_29': 5.234,
     'tbl_30': 5.102,
     'tbl_31': 3.06,
     'tbl_32': 7.974,
     'tbl_33': 7.562,
     'tbl_34': 7.195,
     'tbl_35': 7.044,
     'tbl_36': 8.0,
     'tbl_37': 8.0,
     'tbl_38': 6.19,
     'tbl_13': 4.033}
    for name, (base, spread) in spreads.items():
        noise = np.random.default_rng([zlib.crc32(name.encode()), seed]).standard_normal(out[name].shape)
        drawn = base * np.exp(spread * noise) if base else spread * noise
        out[name] = jnp.asarray(drawn.astype(out[name].dtype))
    for name, factor in factors.items():
        out[name] = (out[name] * factor).astype(out[name].dtype)
    return out
```

```python
from contextlib import ExitStack

import concourse.bass as bass
from concourse import mybir

F32 = mybir.dt.float32
F32R = mybir.dt.float32r
I32 = mybir.dt.int32
ALU = mybir.AluOpType
ACT = mybir.ActivationFunctionType
AX = mybir.AxisListType

P = 128
M = 39
D = 16
S = 128
SHIFTS = (M + 1) // 2
PER = P // M
KT = -(-SHIFTS // PER)
KR = PER * M
WIDE = M + SHIFTS - 1
WINS = PER - 1 + SHIFTS
QUAD = 4
BANK = 4
NB = -(-M // BANK)
RING = 5
SLOTS = QUAD * NB

ACT_BANKS = (0, 3, 5, 7)
BLOCKS = [min(BANK, M - BANK * n) for n in range(NB)]
ACT_BLOCKS = [BLOCKS[n] if n in ACT_BANKS else 0 for n in range(NB)]
DVE_BLOCKS = [0 if n in ACT_BANKS else BLOCKS[n] for n in range(NB)]
NA = sum(ACT_BLOCKS)
NF = sum(DVE_BLOCKS)
ACT_UPTO = [sum(ACT_BLOCKS[:n + 1]) for n in range(NB)]
DVE_UPTO = [sum(DVE_BLOCKS[:n + 1]) for n in range(NB)]
LEAVES = NA + 1
ADDS = 5
SETS = 4
LAG = 2

PAIR = 2 * D
QUADS = PAIR // QUAD
PAIRB = PAIR * NB
EARLY = 9
GATHERS = [(M - 15) * d // EARLY for d in range(EARLY + 1)] + [M - 15 + 15 * (d - EARLY) // (D - EARLY) for d in range(EARLY + 1, D + 1)]


def cin_kernel(nc, tables, ids, dense_t, w1a, w1b, b1, w2, b2, wt1, bt1, wt2, bt2, wt3, out):
    B = ids.shape[0]
    NBLK = B // P
    ITERS = NBLK // 2
    DN = dense_t.shape[0]
    N1 = wt1.shape[1] // P
    N2 = wt2.shape[1] // P
    CH = 512
    NCH = B // CH

    with ExitStack() as ctx:
        def sb(name, shape, dt=F32):
            return ctx.enter_context(nc.sbuf_tensor(name, shape, dt))

        def sem(name):
            return ctx.enter_context(nc.semaphore(name))

        w2h = sb("w2h", [P, M * S], F32R)
        w2l = sb("w2l", [P, M * S], F32R)
        leaves = sb("leaves", [P, SETS, LEAVES, S])
        leaves_flat = leaves[:].rearrange("p a b c -> p (a b c)")
        w2f = leaves_flat[:, 0:M * S]
        w1c = sb("w1c", [P, KT, S])
        w1t = sb("w1t", [P, KT, S])
        ident = sb("ident", [P, P])
        b1c = sb("b1c", [P, 1])
        b2r = sb("b2r", [P, S])
        idx = sb("idx", [P, 2, M], I32)
        emb = sb("emb", [P, 2, M * D])
        x0 = sb("x0", [P, 2, D, WIDE])
        win = sb("win", [P, QUAD, WINS * M])
        fac = sb("fac", [P, 2, QUAD * P])
        pair = sb("pair", [P, KT, QUAD * P])
        x1f = sb("x1f", [P, 2, QUAD * P])
        x1h = sb("x1h", [P, 2, QUAD * P], F32R)
        x1l = sb("x1l", [P, 2, QUAD * P], F32R)
        z1q = sb("z1q", [P, 2, QUAD, P])
        z2p = sb("z2p", [P, 2, S])
        z1 = sb("z1", [P, NBLK, P])
        z2 = sb("z2", [P, NBLK, S])
        wt1s = sb("wt1s", [P, 3, N1 * P])
        wt2s = sb("wt2s", [P, N1, N2 * P])
        wt3s = sb("wt3s", [P, N2])
        bt1s = sb("bt1s", [P, N1])
        bt2s = sb("bt2s", [P, N2])
        dts = sb("dts", [DN, B])
        yrow = pair[0:1, :, :].rearrange("p a b -> p (a b)")[:, 0:B]
        z2t = leaves_flat[:, 0:2 * CH].rearrange("p (a c) -> p a c", a=2)
        h1 = leaves_flat[:, 2 * CH:(2 + 2 * N1) * CH].rearrange("p (a m c) -> p a m c", a=2, m=N1)
        h2 = leaves_flat[:, (2 + 2 * N1) * CH:(2 + 2 * N1 + 2 * N2) * CH].rearrange("p (a m c) -> p a m c", a=2, m=N2)

        ps = ctx.enter_context(nc.psum_tensor("ps", [P, 8, 512], F32))
        TR, X1 = RING, RING + 2

        w1_in = sem("w1_in")
        b_in = sem("b_in")
        mlp_in = sem("mlp_in")
        w2_in = sem("w2_in")
        set_up = sem("set_up")
        w1_zero = sem("w1_zero")
        w1_sum = sem("w1_sum")
        w2_high = sem("w2_high")
        w2_low = sem("w2_low")
        idx_in = [sem("idx_in0"), sem("idx_in1")]
        gathered = [sem("gathered0"), sem("gathered1")]
        x0_set = sem("x0_set")
        win_set = sem("win_set")
        turned = sem("turned")
        fac_set = sem("fac_set")
        pair_set = sem("pair_set")
        x1_sum = sem("x1_sum")
        x1_set = sem("x1_set")
        high_set = sem("high_set")
        low_set = sem("low_set")
        z1q_set = sem("z1q_set")
        z1_set = sem("z1_set")
        bank_full = sem("bank_full")
        fma = sem("fma")
        scaled = sem("scaled")
        tree = sem("tree")
        x2_set = sem("x2_set")
        z1_out = [sem("z1_out0"), sem("z1_out1")]
        z2_out = [sem("z2_out0"), sem("z2_out1")]
        m_turn = sem("m_turn")
        m_z2t = sem("m_z2t")
        m_h1 = sem("m_h1")
        m_r1 = sem("m_r1")
        m_h2 = sem("m_h2")
        m_r2 = sem("m_r2")
        m_y = sem("m_y")
        m_yc = sem("m_yc")
        y_out = sem("y_out")
        z1h = sem("z1h")
        MLP_LOADS = 7

        block = ctx.enter_context(nc.Block())

        def wait(eng, s, it, per, k):
            v = it * per + k
            if isinstance(v, int) and v <= 0:
                return
            eng.wait_ge(s, v)

        def iterations(eng, body):
            body(0, True, False)
            with eng.Fori(1, ITERS - 1) as it:
                body(it, False, False)
            body(ITERS - 1, False, True)

        @block.sync
        def _(sp):
            for u in range(2):
                sp.dma_start(idx[:, u, :], ids[u * P:(u + 1) * P, :]).then_inc(idx_in[u], 16)
            sp.dma_start(w1c[0:KR, :, :], w1a).then_inc(w1_in, 16)
            sp.wait_ge(w1_zero, 1)
            sp.dma_start(w1t[M:KR, 0, :], w1b[M:KR, 0, :]).then_inc(w1_in, 16)
            sp.dma_start(w1t[0:KR, 1:KT, :], w1b[:, 1:KT, :]).then_inc(w1_in, 16)
            sp.dma_start(b1c[:, :], b1.rearrange("(p a) -> p a", a=1)).then_inc(b_in, 16)
            sp.dma_start(w2f, w2).then_inc(w2_in, 16)
            sp.dma_start(b2r[:, :], b2.rearrange("(a s) -> a s", a=1).broadcast_to([P, S])).then_inc(b_in, 16)
            sp.dma_start(wt1s[:, 0:2, :], wt1[0:2 * P, :].rearrange("(k p) n -> p k n", p=P)).then_inc(mlp_in, 16)
            sp.dma_start(wt1s[0:DN, 2, :], wt1[2 * P:2 * P + DN, :]).then_inc(mlp_in, 16)
            sp.dma_start(wt2s[:, :, :], wt2.rearrange("(k p) n -> p k n", p=P)).then_inc(mlp_in, 16)
            sp.dma_start(wt3s[:, :], wt3).then_inc(mlp_in, 16)
            sp.dma_start(bt1s[:, :], bt1).then_inc(mlp_in, 16)
            sp.dma_start(bt2s[:, :], bt2).then_inc(mlp_in, 16)
            sp.dma_start(dts[:, :], dense_t).then_inc(mlp_in, 16)

            def body(it, first, last):
                for u in range(2):
                    if not last:
                        wait(sp, gathered[u], it, 16 * M, 16 * M)
                        sp.dma_start(idx[:, u, :], ids[bass.ds((it * 2 + u + 2) * P, P), :]).then_inc(idx_in[u], 16)

            iterations(sp, body)
            sp.wait_ge(m_yc, NCH)
            sp.dma_start(out.rearrange("b a -> a b"), yrow[:, :]).then_inc(y_out, 16)
            sp.wait_ge(y_out, 16)

        @block.gpsimd
        def _(pool):
            pool.memset(ident[:, :], 0.0).then_inc(set_up, 1)
            pool.wait_ge(set_up, 1)
            pool.affine_select(out=ident[:, :], in_=ident[:, :], compare_op=ALU.not_equal, fill=1.0, base=0,
                               pattern=[[-1, P]], channel_multiplier=1).then_inc(set_up, 1)

            def gather(u, f0, f1):
                for f in range(f0, f1):
                    pool.indirect_dma_start(
                        out=emb[:, u, f * D:(f + 1) * D], out_offset=None, in_=tables[f],
                        in_offset=bass.IndirectOffsetOnAxis(ap=idx[:, u, f:f + 1], axis=0)).then_inc(gathered[u], 16)

            def body(it, first, last):
                for t in range(PAIR):
                    u, d = divmod(t, D)
                    ahead = 1 if d < EARLY else 2
                    blk = u + ahead
                    v = blk % 2
                    if not (last and blk > 1):
                        if d == EARLY:
                            wait(pool, idx_in[v], it, 16, 16 * (blk // 2 + 1))
                            wait(pool, x0_set, it, 2, blk - 1)
                    if d == D - 2:
                        wait(pool, z1q_set, it, QUADS, (u + 1) * 4)
                        wait(pool, z1_set, it, 2, u)
                        pool.tensor_tensor(z1q[:, u, 0:2, :], z1q[:, u, 0:2, :], z1q[:, u, 2:4, :], ALU.add).then_inc(z1h, 1)
                        wait(pool, z1h, it, 2, u + 1)
                        pool.tensor_tensor(z1q[:, u, 0, :], z1q[:, u, 0, :], z1q[:, u, 1, :], ALU.add).then_inc(z1_set, 1)
                    r = t % SETS
                    wait(pool, scaled, it, PAIR * NA, (t + 1) * NA)
                    wait(pool, fma, it, PAIR * NF, (t + 1) * NF)
                    steps = [(leaves[:, r, 0:8, :], leaves[:, r, 8:16, :]),
                             (leaves[:, r, 0:4, :], leaves[:, r, 4:8, :]),
                             (leaves[:, r, 0:2, :], leaves[:, r, 2:4, :]),
                             (leaves[:, r, 0, :], leaves[:, r, 1, :]),
                             (leaves[:, r, 0, :], leaves[:, r, 16, :])]
                    for k, (a, b) in enumerate(steps):
                        if k:
                            wait(pool, tree, it, PAIR * ADDS, t * ADDS + k)
                        pool.tensor_tensor(a, a, b, ALU.add).then_inc(tree, 1)
                    if not (last and blk > 1):
                        done = M - 15 if ahead == 2 else -15
                        gather(v, GATHERS[d] - done, GATHERS[d + 1] - done)

            pool.wait_ge(idx_in[0], 16)
            gather(0, 0, M)
            pool.wait_ge(idx_in[1], 16)
            gather(1, 0, 15)
            iterations(pool, body)

        @block.scalar
        def _(act):
            def arrange(it, u, blk):
                wait(act, gathered[u], it, 16 * M, 16 * M * (blk // 2 + 1))
                wait(act, fma, it, PAIR * NF, (blk - 1) * D * NF)
                src = emb[:, u, :].rearrange("p (f d) -> p d f", d=D)
                act.copy(x0[:, u, :, 0:M], src)
                act.copy(x0[:, u, :, M:WIDE], src[:, :, 0:WIDE - M]).then_inc(x0_set, 1)

            def windows(it, q, i):
                blk, quad = divmod(q, 4)
                if i == 0:
                    wait(act, x0_set, it, 2, blk + 1)
                    wait(act, turned, it, QUADS * (KT + 1), q * (KT + 1))
                x = x0[:, blk % 2, quad * QUAD + i, 0:1]
                row = [list(e) for e in x.ap][0]
                src = [bass.AP(tensor=x.tensor, offset=x.offset, ap=[row, [step, n], [1, M]])
                       for step, n in ((0, PER - 1), (1, SHIFTS))]
                act.copy(win[:, i, 0:(PER - 1) * M].rearrange("p (k i) -> p k i", i=M), src[0]).then_inc(win_set, 1)
                act.copy(win[:, i, (PER - 1) * M:].rearrange("p (k i) -> p k i", i=M), src[1]).then_inc(win_set, 1)

            def factor(it, q):
                wait(act, turned, it, QUADS * (KT + 1), q * (KT + 1) + 1)
                wait(act, pair_set, it, QUADS * KT, (q - 1) * KT)
                act.copy(fac[0:KR, q % 2, :], ps[0:KR, TR, :]).then_inc(fac_set, 1)

            def relu_x1(it, q):
                wait(act, x1_sum, it, QUADS, q + 1)
                wait(act, z1q_set, it, QUADS, q - 1)
                act.activation(x1f[:, q % 2, :], ps[:, X1, :], ACT.Relu, bias=b1c[:, :]).then_inc(x1_set, 1)
                wait(act, x1_set, it, QUADS, q + 1)
                wait(act, bank_full, it, PAIRB, (q - 1) * SLOTS)
                act.copy(x1h[:, q % 2, :], x1f[:, q % 2, :]).then_inc(high_set, 1)

            def keep_sums(it, blk):
                u = blk % 2
                wait(act, z1_set, it, 2, blk + 1)
                act.dma_start(z1[:, bass.ds(it * 2 + blk, 1), :], z1q[:, u, 0:1, :]).then_inc(z1_out[u], 16)
                wait(act, x2_set, it, PAIR, (blk + 1) * D)
                act.dma_start(z2[:, bass.ds(it * 2 + blk, 1), :], z2p[:, u:u + 1, :]).then_inc(z2_out[u], 16)

            def body(it, first, last):
                for t in range(PAIR):
                    u, d = divmod(t, D)
                    r = t % SETS
                    if d == 3 and not (first and u == 0):
                        keep_sums(it, u - 1)
                    wait(act, x2_set, it, PAIR, t - SETS + 1)
                    for n in range(NB):
                        if ACT_BLOCKS[n]:
                            wait(act, bank_full, it, PAIRB, t * NB + n + 1)
                        for k in range(ACT_BLOCKS[n]):
                            a = (ACT_UPTO[n - 1] if n else 0) + k
                            m = n * BANK + k
                            slot = LEAVES - 1 if a == 0 else a - 1
                            act.activation(leaves[:, r, slot, :], ps[:, n % RING, k * S:(k + 1) * S], ACT.Copy,
                                           scale=x0[:, u, d, m:m + 1]).then_inc(scaled, 1)
                        s = (t % QUAD) * NB + n
                        q = t // QUAD + 1
                        if d == EARLY and n == 5 and not (last and u == 1):
                            arrange(it, (u + 1) % 2, u + 1)
                        if s in range(26, 38, 3) and not (last and q + 1 >= QUADS):
                            windows(it, q + 1, (s - 26) // 3)
                        if last and q == QUADS:
                            continue
                        if s == 2:
                            factor(it, q)
                        if s == 30:
                            relu_x1(it, q)

            act.wait_ge(w2_in, 16)
            act.copy(w2h[:, :], w2f).then_inc(w2_high, 1)
            arrange(0, 0, 0)
            act.wait_ge(b_in, 32)
            for i in range(QUAD):
                windows(0, 0, i)
            factor(0, 0)
            for i in range(QUAD):
                windows(0, 1, i)
            relu_x1(0, 0)
            act.wait_ge(w2_low, 1)
            iterations(act, body)
            keep_sums(ITERS - 1, 1)

            def relu_h2(n):
                for m in range(N2):
                    act.wait_ge(m_h2, n * N2 + m + 1)
                    if n >= 2:
                        act.wait_ge(m_y, n - 1)
                    act.activation(h2[:, n % 2, m, :], ps[:, TR + m, :], ACT.Relu, bias=bt2s[:, m:m + 1]).then_inc(m_r2, 1)

            for n in range(NCH):
                for m in range(N1):
                    act.wait_ge(m_h1, n * N1 + m + 1)
                    if n >= 2:
                        act.wait_ge(m_h2, (n - 1) * N2)
                    act.activation(h1[:, n % 2, m, :], ps[:, m, :], ACT.Relu, bias=bt1s[:, m:m + 1]).then_inc(m_r1, 1)
                if n:
                    relu_h2(n - 1)
            relu_h2(NCH - 1)

        @block.vector
        def _(dve):
            def multiply(it, q, t):
                rows = KR if t < KT - 1 else (SHIFTS - PER * (KT - 1)) * M
                wait(dve, turned, it, QUADS * (KT + 1), q * (KT + 1) + t + 2)
                if t == 0:
                    wait(dve, fac_set, it, QUADS, q + 1)
                    wait(dve, x1_sum, it, QUADS, q)
                dve.tensor_tensor(pair[0:rows, t, :], ps[0:rows, TR + (t + 1) % 2, :], fac[0:rows, q % 2, :],
                                  ALU.mult).then_inc(pair_set, 1)

            def split_x1(it, q):
                blk, quad = divmod(q, 4)
                wait(dve, high_set, it, QUADS, q + 1)
                wait(dve, bank_full, it, PAIRB, (q - 1) * SLOTS)
                dve.tensor_tensor(x1l[:, q % 2, :], x1f[:, q % 2, :], x1h[:, q % 2, :].bitcast(F32),
                                  ALU.subtract).then_inc(low_set, 1)
                if quad == 0:
                    wait(dve, z1_out[blk % 2], it, 16, 16 * (blk // 2))
                dve.tensor_reduce(z1q[:, blk % 2, quad, :], x1f[:, q % 2, :].rearrange("p (d b) -> p b d", d=QUAD),
                                  AX.X, ALU.add).then_inc(z1q_set, 1)

            def finish(it, t):
                blk, d = divmod(t, D)
                wait(dve, tree, it, PAIR * ADDS, (t + 1) * ADDS)
                total, acc = leaves[:, t % SETS, 0, :], z2p[:, blk % 2, :]
                if d == 0:
                    wait(dve, z2_out[blk % 2], it, 16, 16 * (blk // 2))
                    dve.tensor_scalar(acc, total, 0.0, None, ALU.max).then_inc(x2_set, 1)
                else:
                    wait(dve, x2_set, it, PAIR, t)
                    dve.scalar_tensor_tensor(out=acc, in0=total, scalar=0.0, in1=acc, op0=ALU.max,
                                             op1=ALU.add).then_inc(x2_set, 1)

            def body(it, first, last):
                for t in range(PAIR):
                    u, d = divmod(t, D)
                    r = t % SETS
                    for n in range(NB):
                        if DVE_BLOCKS[n]:
                            wait(dve, bank_full, it, PAIRB, t * NB + n + 1)
                        for k in range(DVE_BLOCKS[n]):
                            f = (DVE_UPTO[n - 1] if n else 0) + k
                            m = n * BANK + k
                            own = leaves[:, r, LEAVES - 2 + f % 2, :]
                            start = own
                            if f == 0:
                                start = b2r[:, :]
                            elif f == 1:
                                wait(dve, scaled, it, PAIR * NA, t * NA + 1)
                            else:
                                wait(dve, fma, it, PAIR * NF, t * NF + f - 1)
                            dve.scalar_tensor_tensor(out=own, in0=ps[:, n % RING, k * S:(k + 1) * S],
                                                     scalar=x0[:, u, d, m:m + 1], in1=start,
                                                     op0=ALU.mult, op1=ALU.add).then_inc(fma, 1)
                        s = (t % QUAD) * NB + n
                        q = t // QUAD + 1
                        if n == 5 and not (first and t < LAG):
                            finish(it, t - LAG)
                        if last and q == QUADS:
                            continue
                        if s in range(5, 5 + 3 * KT, 3):
                            multiply(it, q, (s - 5) // 3)
                        if s == 31:
                            split_x1(it, q)
                if last:
                    for t in range(PAIR - LAG, PAIR):
                        finish(it, t)

            dve.memset(w1t[0:KR, 0, :], 0.0).then_inc(w1_zero, 1)
            dve.wait_ge(w1_in, 48)
            dve.tensor_tensor(w1c[0:KR, :, :], w1c[0:KR, :, :], w1t[0:KR, :, :], ALU.add).then_inc(w1_sum, 1)
            dve.wait_ge(w2_high, 1)
            dve.tensor_tensor(w2l[:, :], w2f, w2h[:, :].bitcast(F32), ALU.subtract).then_inc(w2_low, 1)
            dve.wait_ge(b_in, 32)
            for t in range(KT):
                multiply(0, 0, t)
            split_x1(0, 0)
            iterations(dve, body)

            def copy_y(n):
                dve.wait_ge(m_y, n + 1)
                dve.tensor_copy(yrow[0:1, n * CH:(n + 1) * CH], ps[0:1, X1, :]).then_inc(m_yc, 1)

            dve.wait_ge(z2_out[0], 16 * ITERS)
            dve.wait_ge(z2_out[1], 16 * ITERS)
            for n in range(NCH):
                dve.wait_ge(m_turn, n + 1)
                if n >= 2:
                    dve.wait_ge(m_h1, (n - 1) * N1)
                dve.tensor_copy(z2t[:, n % 2, :], ps[:, 4, :]).then_inc(m_z2t, 1)
                if n:
                    copy_y(n - 1)
            copy_y(NCH - 1)

        @block.tensor
        def _(pe):
            def turn(it, q, g):
                if g == 0:
                    wait(pe, win_set, it, QUADS * QUAD * 2, (q + 1) * QUAD * 2)
                if g < 2:
                    wait(pe, pair_set, it, QUADS * KT, (q - 1) * KT + KT - 1 + g)
                elif g == 2:
                    wait(pe, fac_set, it, QUADS, q + 1)
                else:
                    wait(pe, pair_set, it, QUADS * KT, q * KT + g - 2)
                first = 0 if g == 0 else PER * g - 1
                n = min(PER, WINS - first)
                for i in range(QUAD):
                    mm = pe.transpose(ps[0:n * M, TR + g % 2, i * P:(i + 1) * P], win[:, i, first * M:(first + n) * M],
                                      ident[:, :])
                mm.then_inc(turned, 1)

            def contract(it, q, t):
                rows = KR if t < KT - 1 else (SHIFTS - PER * (KT - 1)) * M
                wait(pe, pair_set, it, QUADS * KT, q * KT + t + 1)
                if t == 0:
                    wait(pe, x1_set, it, QUADS, q)
                mm = pe.matmul(ps[:, X1, :], w1c[0:rows, t, :], pair[0:rows, t, :], start=(t == 0), stop=(t == KT - 1))
                if t == KT - 1:
                    mm.then_inc(x1_sum, 1)

            def body(it, first, last):
                for t in range(PAIR):
                    for n in range(NB):
                        s = (t % QUAD) * NB + n
                        q = t // QUAD + 1
                        if not (last and q == QUADS):
                            if s in range(1, 1 + 3 * (KT + 1), 3):
                                turn(it, q, (s - 1) // 3)
                            if s in range(10, 10 + 3 * KT, 3):
                                contract(it, q, (s - 10) // 3)
                        if s == 0:
                            wait(pe, low_set, it, QUADS, q)
                            wait(pe, high_set, it, QUADS, q)
                        g = t * NB + n - RING
                        tt, nn = divmod(g, NB)
                        if nn in ACT_BANKS:
                            wait(pe, scaled, it, PAIR * NA, tt * NA + ACT_UPTO[nn])
                        else:
                            wait(pe, fma, it, PAIR * NF, tt * NF + DVE_UPTO[nn])
                        par, at = (t // QUAD) % 2, (t % QUAD) * P
                        hi, lo = x1h[:, par, at:at + P], x1l[:, par, at:at + P]
                        w = slice(n * BANK * S, (n * BANK + BLOCKS[n]) * S)
                        dst = ps[:, n % RING, 0:BLOCKS[n] * S]
                        pe.matmul(dst, hi, w2h[:, w], start=True, stop=False)
                        pe.matmul(dst, hi, w2l[:, w], start=False, stop=False)
                        pe.matmul(dst, lo, w2h[:, w], start=False, stop=True).then_inc(bank_full, 1)

            pe.wait_ge(set_up, 2)
            pe.wait_ge(w1_sum, 1)
            for g in range(KT + 1):
                turn(0, 0, g)
            for t in range(KT):
                contract(0, 0, t)
            pe.wait_ge(w2_low, 1)
            iterations(pe, body)

            pe.wait_ge(x2_set, NBLK * D)
            pe.wait_ge(mlp_in, 16 * MLP_LOADS)
            for u in range(2):
                pe.wait_ge(z1_out[u], 16 * ITERS)
                pe.wait_ge(z2_out[u], 16 * ITERS)

            def upper(n):
                pe.wait_ge(m_r1, (n + 1) * N1)
                for m in range(N2):
                    if n:
                        pe.wait_ge(m_r2, (n - 1) * N2 + m + 1)
                    for k in range(N1):
                        mm = pe.matmul(ps[:, TR + m, :], wt2s[:, k, m * P:(m + 1) * P], h1[:, n % 2, k, :],
                                       start=(k == 0), stop=(k == N1 - 1))
                    mm.then_inc(m_h2, 1)
                pe.wait_ge(m_r2, (n + 1) * N2)
                if n:
                    pe.wait_ge(m_yc, n)
                for k in range(N2):
                    mm = pe.matmul(ps[0:1, X1, :], wt3s[:, k:k + 1], h2[:, n % 2, k, :], start=(k == 0), stop=(k == N2 - 1))
                mm.then_inc(m_y, 1)

            for n in range(NCH):
                if n:
                    pe.wait_ge(m_z2t, n)
                for i in range(CH // P):
                    mm = pe.transpose(ps[:, 4, i * P:(i + 1) * P], z2[:, n * (CH // P) + i, :], ident[:, :])
                mm.then_inc(m_turn, 1)
                pe.wait_ge(m_z2t, n + 1)
                zin = [(wt1s[:, 0, :], z1[:, n * (CH // P):(n + 1) * (CH // P), :]),
                       (wt1s[:, 1, :], z2t[:, n % 2, :]),
                       (wt1s[0:DN, 2, :], dts[:, n * CH:(n + 1) * CH])]
                for m in range(N1):
                    if n:
                        pe.wait_ge(m_r1, (n - 1) * N1 + m + 1)
                    for k, (w, x) in enumerate(zin):
                        mm = pe.matmul(ps[:, m, :], w[:, m * P:(m + 1) * P], x, start=(k == 0), stop=(k == 2))
                    mm.then_inc(m_h1, 1)
                if n:
                    upper(n - 1)
            upper(NCH - 1)


def kernel(**inputs):
    import numpy as np
    import concourse.bacc as bacc
    from concourse.bass_utils import run_bass_kernel_spmd

    a = {k: np.asarray(v) for k, v in inputs.items()}
    i = np.tile(np.arange(M), PER)[:, None]
    k = (np.arange(KR) // M)[:, None] + PER * np.arange(KT)[None, :]
    j = (i + k) % M
    i = np.broadcast_to(i, j.shape)
    w1 = a["L0_rec_W1"].transpose(1, 2, 0)
    arrays = {f"tbl_{f}": a[f"tbl_{f}"] for f in range(M)}
    arrays |= {
        "ids": a["ids"], "dense_t": a["dense_ctx"].T, "w1a": w1[i, j], "w1b": w1[j, i], "b1": a["L0_rec_b1"],
        "w2": a["L0_rec_W2"].transpose(1, 2, 0).reshape(S, M * S), "b2": a["L0_rec_b2"],
        "wt1": a["W_top1"], "bt1": a["b_top1"].reshape(-1, P).T, "wt2": a["W_top2"],
        "bt2": a["b_top2"].reshape(-1, P).T, "wt3": a["W_top3"].reshape(-1, P).T,
    }
    arrays = {n: np.ascontiguousarray(x) for n, x in arrays.items()}
    nc = bacc.Bacc("TRN2", target_bir_lowering=False, num_devices=1)
    ap = {n: nc.dram_tensor(n, x.shape, mybir.dt.from_np(x.dtype), kind="ExternalInput").ap() for n, x in arrays.items()}
    out = nc.dram_tensor("y", (a["ids"].shape[0], 1), F32, kind="ExternalOutput").ap()
    tables = [ap[f"tbl_{f}"] for f in range(M)]
    cin_kernel(nc, tables, *(ap[n] for n in ("ids", "dense_t", "w1a", "w1b", "b1", "w2", "b2", "wt1", "bt1", "wt2",
                                             "bt2", "wt3")), out)
    r = run_bass_kernel_spmd(nc, [arrays], core_ids=[0])
    return r.results[0]["y"]
```

```python
from contextlib import ExitStack

import concourse.bass as bass
from concourse import mybir

F32 = mybir.dt.float32
F32R = mybir.dt.float32r
I32 = mybir.dt.int32
ALU = mybir.AluOpType
ACT = mybir.ActivationFunctionType
AX = mybir.AxisListType

P = 128
M = 39
D = 16
S = 128
SHIFTS = (M + 1) // 2
PER = P // M
KT = -(-SHIFTS // PER)
KR = PER * M
WIDE = M + SHIFTS - 1
LOW = 64
TURNED = LOW + 1
XR = LOW + WIDE
USES = KT + 2
QUAD = 4
BANK = 4
NB = -(-M // BANK)
RING = 5
SLOTS = QUAD * NB

ACT_BANKS = (0, 3, 5, 7)
BLOCKS = [min(BANK, M - BANK * n) for n in range(NB)]
ACT_BLOCKS = [BLOCKS[n] if n in ACT_BANKS else 0 for n in range(NB)]
DVE_BLOCKS = [0 if n in ACT_BANKS else BLOCKS[n] for n in range(NB)]
NA = sum(ACT_BLOCKS)
NF = sum(DVE_BLOCKS)
ACT_UPTO = [sum(ACT_BLOCKS[:n + 1]) for n in range(NB)]
DVE_UPTO = [sum(DVE_BLOCKS[:n + 1]) for n in range(NB)]
LEAVES = NA + 1
ADDS = 5
SETS = 4
LAG = 2

PAIR = 2 * D
QUADS = PAIR // QUAD
PAIRB = PAIR * NB
EARLY = 8
GATHERS = [(M - 15) * d // EARLY for d in range(EARLY + 1)] + [M - 15 + 15 * (d - EARLY) // (D - EARLY) for d in range(EARLY + 1, D + 1)]


def cin_kernel(nc, tables, ids, dense_t, sel, w1a, w1b, b1, w2, b2, wt1, bt1, wt2, bt2, wt3, out):
    B = ids.shape[0]
    NBLK = B // P
    ITERS = NBLK // 2
    DN = dense_t.shape[0]
    N1 = wt1.shape[1] // P
    N2 = wt2.shape[1] // P

    with ExitStack() as ctx:
        def sb(name, shape, dt=F32):
            return ctx.enter_context(nc.sbuf_tensor(name, shape, dt))

        def sem(name):
            return ctx.enter_context(nc.semaphore(name))

        w2h = sb("w2h", [P, M * S], F32R)
        w2l = sb("w2l", [P, M * S], F32R)
        leaves = sb("leaves", [P, SETS, LEAVES, S])
        leaves_flat = leaves[:].rearrange("p a b c -> p (a b c)")
        w2f = leaves_flat[:, 0:M * S]
        w1c = sb("w1c", [P, KT, S])
        w1t = sb("w1t", [P, KT, S])
        ident = sb("ident", [P, P])
        b1c = sb("b1c", [P, 1])
        b2r = sb("b2r", [P, S])
        idx = sb("idx", [P, 2, M], I32)
        emb = sb("emb", [P, 2, M * D])
        x0 = sb("x0", [P, 2, D, TURNED])
        xs = sb("xs", [XR, QUAD * P], F32R)
        sels = sb("sels", [XR, (KT + 1) * KR], F32R)
        self_ = sb("self", [XR, (KT + 1) * KR])
        fac = sb("fac", [P, 2, QUAD * P])
        pair = sb("pair", [P, KT, QUAD * P])
        x1f = sb("x1f", [P, 2, QUAD * P])
        x1h = sb("x1h", [P, 2, QUAD * P], F32R)
        x1l = sb("x1l", [P, 2, QUAD * P], F32R)
        z1q = sb("z1q", [P, 2, QUAD, P])
        z2p = sb("z2p", [P, 2, S])
        wt1s = sb("wt1s", [P, 3, N1 * P])
        wt2s = sb("wt2s", [P, N1, N2 * P])
        wt3s = sb("wt3s", [P, N2])
        bt1s = sb("bt1s", [P, N1])
        bt2s = sb("bt2s", [P, N2])
        dts = sb("dts", [DN, 2, P])
        z2t = sb("z2t", [S, P])
        h1 = sb("h1", [P, N1, P])
        h2 = sb("h2", [P, N2, P])
        yrow = sb("yrow", [1, 2, P])

        ps = ctx.enter_context(nc.psum_tensor("ps", [P, 8, 512], F32))
        TR, X1 = RING, RING + 2

        w1_in = sem("w1_in")
        b_in = sem("b_in")
        mlp_in = sem("mlp_in")
        w2_in = sem("w2_in")
        set_up = sem("set_up")
        w1_zero = sem("w1_zero")
        xs_zero = sem("xs_zero")
        w1_sum = sem("w1_sum")
        w2_high = sem("w2_high")
        w2_low = sem("w2_low")
        idx_in = [sem("idx_in0"), sem("idx_in1")]
        gathered = [sem("gathered0"), sem("gathered1")]
        x0_set = sem("x0_set")
        sel_in = sem("sel_in")
        sel_set = sem("sel_set")
        dense_in = [sem("dense_in0"), sem("dense_in1")]
        hi0_set = sem("hi0_set")
        lo0_set = sem("lo0_set")
        turned = sem("turned")
        fac_set = sem("fac_set")
        pair_set = sem("pair_set")
        x1_sum = sem("x1_sum")
        x1_set = sem("x1_set")
        high_set = sem("high_set")
        low_set = sem("low_set")
        z1q_set = sem("z1q_set")
        z1_set = sem("z1_set")
        bank_full = sem("bank_full")
        fma = sem("fma")
        scaled = sem("scaled")
        tree = sem("tree")
        x2_set = sem("x2_set")
        m_turn = sem("m_turn")
        m_z2t = sem("m_z2t")
        m_h1 = sem("m_h1")
        m_r1 = sem("m_r1")
        m_h2 = sem("m_h2")
        m_r2 = sem("m_r2")
        m_y = sem("m_y")
        m_yc = sem("m_yc")
        y_out = [sem("y_out0"), sem("y_out1")]
        z1h = sem("z1h")
        MLP_LOADS = 6

        block = ctx.enter_context(nc.Block())

        def wait(eng, s, it, per, k):
            v = it * per + k
            if isinstance(v, int) and v <= 0:
                return
            eng.wait_ge(s, v)

        def iterations(eng, body):
            body(0, True, False)
            with eng.Fori(1, ITERS - 1) as it:
                body(it, False, False)
            body(ITERS - 1, False, True)

        def z2_bank(blk):
            return ((4 * blk + 5) * USES + USES - 1) % 2

        out_rows = out.rearrange("(k b) a -> k (b a)", b=P)

        @block.sync
        def _(sp):
            for u in range(2):
                sp.dma_start(idx[:, u, :], ids[u * P:(u + 1) * P, :]).then_inc(idx_in[u], 16)
            sp.dma_start(self_[:, :], sel).then_inc(sel_in, 16)
            for u in range(2):
                sp.dma_start(dts[:, u, :], dense_t[:, u * P:(u + 1) * P]).then_inc(dense_in[u], 16)
            sp.dma_start(w1c[0:KR, :, :], w1a).then_inc(w1_in, 16)
            sp.wait_ge(w1_zero, 1)
            sp.dma_start(w1t[M:KR, 0, :], w1b[M:KR, 0, :]).then_inc(w1_in, 16)
            sp.dma_start(w1t[0:KR, 1:KT, :], w1b[:, 1:KT, :]).then_inc(w1_in, 16)
            sp.dma_start(b1c[:, :], b1.rearrange("(p a) -> p a", a=1)).then_inc(b_in, 16)
            sp.dma_start(w2f, w2).then_inc(w2_in, 16)
            sp.dma_start(b2r[:, :], b2.rearrange("(a s) -> a s", a=1).broadcast_to([P, S])).then_inc(b_in, 16)
            sp.dma_start(wt1s[:, 0:2, :], wt1[0:2 * P, :].rearrange("(k p) n -> p k n", p=P)).then_inc(mlp_in, 16)
            sp.dma_start(wt1s[0:DN, 2, :], wt1[2 * P:2 * P + DN, :]).then_inc(mlp_in, 16)
            sp.dma_start(wt2s[:, :, :], wt2.rearrange("(k p) n -> p k n", p=P)).then_inc(mlp_in, 16)
            sp.dma_start(wt3s[:, :], wt3).then_inc(mlp_in, 16)
            sp.dma_start(bt1s[:, :], bt1).then_inc(mlp_in, 16)
            sp.dma_start(bt2s[:, :], bt2).then_inc(mlp_in, 16)

            def body(it, first, last):
                for u in range(2):
                    if not first or u == 1:
                        blk = u - 1
                        v = blk % 2
                        wait(sp, m_yc, it, 2, blk + 1)
                        sp.dma_start(out_rows[bass.ds(it * 2 + blk, 1), :], yrow[0:1, v, :]).then_inc(y_out[v], 16)
                        if not (last and u == 1):
                            sp.dma_start(dts[:, v, :], dense_t[:, bass.ds((it * 2 + blk + 2) * P, P)]).then_inc(dense_in[v], 16)
                    if not last:
                        wait(sp, gathered[u], it, 16 * M, 16 * M)
                        sp.dma_start(idx[:, u, :], ids[bass.ds((it * 2 + u + 2) * P, P), :]).then_inc(idx_in[u], 16)

            iterations(sp, body)
            sp.wait_ge(m_yc, NBLK)
            sp.dma_start(out_rows[NBLK - 1:NBLK, :], yrow[0:1, 1, :]).then_inc(y_out[1], 16)
            for u in range(2):
                sp.wait_ge(y_out[u], 16 * ITERS)

        @block.gpsimd
        def _(pool):
            pool.memset(ident[:, :], 0.0).then_inc(set_up, 1)
            pool.wait_ge(set_up, 1)
            pool.affine_select(out=ident[:, :], in_=ident[:, :], compare_op=ALU.not_equal, fill=1.0, base=0,
                               pattern=[[-1, P]], channel_multiplier=1).then_inc(set_up, 1)

            def gather(u, f0, f1):
                for f in range(f0, f1):
                    pool.indirect_dma_start(
                        out=emb[:, u, f * D:(f + 1) * D], out_offset=None, in_=tables[f],
                        in_offset=bass.IndirectOffsetOnAxis(ap=idx[:, u, f:f + 1], axis=0)).then_inc(gathered[u], 16)

            def body(it, first, last):
                for t in range(PAIR):
                    u, d = divmod(t, D)
                    ahead = 1 if d < EARLY else 2
                    blk = u + ahead
                    v = blk % 2
                    if not (last and blk > 1):
                        if d == EARLY:
                            wait(pool, idx_in[v], it, 16, 16 * (blk // 2 + 1))
                            wait(pool, x0_set, it, 2, blk - 1)
                    if d == D - 2:
                        wait(pool, z1q_set, it, QUADS, (u + 1) * 4)
                        wait(pool, z1_set, it, 2, u)
                        pool.tensor_tensor(z1q[:, u, 0:2, :], z1q[:, u, 0:2, :], z1q[:, u, 2:4, :], ALU.add).then_inc(z1h, 1)
                        wait(pool, z1h, it, 2, u + 1)
                        pool.tensor_tensor(z1q[:, u, 0, :], z1q[:, u, 0, :], z1q[:, u, 1, :], ALU.add).then_inc(z1_set, 1)
                    r = t % SETS
                    wait(pool, scaled, it, PAIR * NA, (t + 1) * NA)
                    wait(pool, fma, it, PAIR * NF, (t + 1) * NF)
                    steps = [(leaves[:, r, 0:8, :], leaves[:, r, 8:16, :]),
                             (leaves[:, r, 0:4, :], leaves[:, r, 4:8, :]),
                             (leaves[:, r, 0:2, :], leaves[:, r, 2:4, :]),
                             (leaves[:, r, 0, :], leaves[:, r, 1, :]),
                             (leaves[:, r, 0, :], leaves[:, r, 16, :])]
                    for k, (a, b) in enumerate(steps):
                        if k:
                            wait(pool, tree, it, PAIR * ADDS, t * ADDS + k)
                        pool.tensor_tensor(a, a, b, ALU.add).then_inc(tree, 1)
                    if not (last and blk > 1):
                        done = M - 15 if ahead == 2 else -15
                        gather(v, GATHERS[d] - done, GATHERS[d + 1] - done)

            pool.wait_ge(idx_in[0], 16)
            gather(0, 0, M)
            pool.wait_ge(idx_in[1], 16)
            gather(1, 0, 15)
            iterations(pool, body)

        @block.scalar
        def _(act):
            def arrange(it, u, blk):
                wait(act, gathered[u], it, 16 * M, 16 * M * (blk // 2 + 1))
                wait(act, fma, it, PAIR * NF, (blk - 1) * D * NF)
                src = emb[:, u, :].rearrange("p (f d) -> p d f", d=D)
                act.copy(x0[:, u, :, 0:M], src)
                act.copy(x0[:, u, :, M:TURNED], src[:, :, 0:TURNED - M]).then_inc(x0_set, 1)

            def high_x0(it, q):
                wait(act, turned, it, QUADS * USES, q * USES + 1)
                act.copy(xs[0:WIDE, :], ps[0:WIDE, TR + q * USES % 2, :]).then_inc(hi0_set, 1)

            def factor(it, q):
                wait(act, turned, it, QUADS * USES, q * USES + 2)
                wait(act, pair_set, it, QUADS * KT, (q - 1) * KT)
                act.copy(fac[0:KR, q % 2, :], ps[0:KR, TR + (q * USES + 1) % 2, :]).then_inc(fac_set, 1)

            def relu_x1(it, q):
                wait(act, x1_sum, it, QUADS, q + 1)
                wait(act, z1q_set, it, QUADS, q - 1)
                act.activation(x1f[:, q % 2, :], ps[:, X1, :], ACT.Relu, bias=b1c[:, :]).then_inc(x1_set, 1)
                wait(act, x1_set, it, QUADS, q + 1)
                wait(act, bank_full, it, PAIRB, (q - 1) * SLOTS)
                act.copy(x1h[:, q % 2, :], x1f[:, q % 2, :]).then_inc(high_set, 1)

            def relu_h1(it, blk):
                wait(act, m_h1, it, 2, blk + 1)
                for m in range(N1):
                    act.activation(h1[:, m, :], ps[:, X1, m * P:(m + 1) * P], ACT.Relu, bias=bt1s[:, m:m + 1]).then_inc(m_r1, 1)

            def relu_h2(it, blk):
                wait(act, m_h2, it, 2, blk + 1)
                for m in range(N2):
                    act.activation(h2[:, m, :], ps[:, X1, m * P:(m + 1) * P], ACT.Relu, bias=bt2s[:, m:m + 1]).then_inc(m_r2, 1)

            def copy_y(it, blk):
                wait(act, m_y, it, 2, blk + 1)
                wait(act, y_out[blk % 2], it, 16, 16 * (blk // 2))
                act.copy(yrow[0:1, blk % 2, :], ps[0:1, X1, 0:P]).then_inc(m_yc, 1)

            def body(it, first, last):
                for t in range(PAIR):
                    u, d = divmod(t, D)
                    r = t % SETS
                    wait(act, x2_set, it, PAIR, t - SETS + 1)
                    for n in range(NB):
                        if ACT_BLOCKS[n]:
                            wait(act, bank_full, it, PAIRB, t * NB + n + 1)
                        for k in range(ACT_BLOCKS[n]):
                            a = (ACT_UPTO[n - 1] if n else 0) + k
                            m = n * BANK + k
                            slot = LEAVES - 1 if a == 0 else a - 1
                            act.activation(leaves[:, r, slot, :], ps[:, n % RING, k * S:(k + 1) * S], ACT.Copy,
                                           scale=x0[:, u, d, m:m + 1]).then_inc(scaled, 1)
                        s = (t % QUAD) * NB + n
                        q = t // QUAD + 1
                        if d == EARLY + 2 and n == 8 and not (last and u == 1):
                            arrange(it, (u + 1) % 2, u + 1)
                        if s == 34 and not (last and q + 1 >= QUADS):
                            high_x0(it, q + 1)
                        if not (first and u == 0):
                            if (q % 4, s) == (1, 36):
                                relu_h1(it, u - 1)
                            if (q % 4, s) == (2, 2):
                                relu_h2(it, u - 1)
                            if (q % 4, s) == (2, 6):
                                copy_y(it, u - 1)
                        if last and q == QUADS:
                            continue
                        if s == 2:
                            factor(it, q)
                        if s == 30:
                            relu_x1(it, q)

            act.wait_ge(sel_in, 16)
            act.copy(sels[:, :], self_[:, :]).then_inc(sel_set, 1)
            act.wait_ge(w2_in, 16)
            act.copy(w2h[:, :], w2f).then_inc(w2_high, 1)
            act.wait_ge(b_in, 32)
            act.wait_ge(xs_zero, 1)
            arrange(0, 0, 0)
            high_x0(0, 0)
            factor(0, 0)
            high_x0(0, 1)
            relu_x1(0, 0)
            act.wait_ge(w2_low, 1)
            act.wait_ge(mlp_in, 16 * MLP_LOADS)
            iterations(act, body)
            relu_h1(ITERS - 1, 1)
            relu_h2(ITERS - 1, 1)
            copy_y(ITERS - 1, 1)

        @block.vector
        def _(dve):
            def multiply(it, q, t):
                rows = KR if t < KT - 1 else (SHIFTS - PER * (KT - 1)) * M
                wait(dve, turned, it, QUADS * USES, q * USES + t + 3)
                if t == 0:
                    wait(dve, fac_set, it, QUADS, q + 1)
                    wait(dve, x1_sum, it, QUADS, q)
                dve.tensor_tensor(pair[0:rows, t, :], ps[0:rows, TR + (q * USES + t + 2) % 2, :], fac[0:rows, q % 2, :],
                                  ALU.mult).then_inc(pair_set, 1)

            def low_x0(it, q):
                wait(dve, hi0_set, it, QUADS, q + 1)
                dve.tensor_tensor(xs[LOW:XR, :], ps[0:WIDE, TR + q * USES % 2, :], xs[0:WIDE, :].bitcast(F32),
                                  ALU.subtract).then_inc(lo0_set, 1)

            def split_x1(it, q):
                blk, quad = divmod(q, 4)
                wait(dve, high_set, it, QUADS, q + 1)
                wait(dve, bank_full, it, PAIRB, (q - 1) * SLOTS)
                dve.tensor_tensor(x1l[:, q % 2, :], x1f[:, q % 2, :], x1h[:, q % 2, :].bitcast(F32),
                                  ALU.subtract).then_inc(low_set, 1)

            def sum_x1(it, q):
                blk, quad = divmod(q, 4)
                if quad == 0:
                    wait(dve, m_h1, it, 2, blk - 1)
                dve.tensor_reduce(z1q[:, blk % 2, quad, :], x1f[:, q % 2, :].rearrange("p (d b) -> p b d", d=QUAD),
                                  AX.X, ALU.add).then_inc(z1q_set, 1)

            def finish(it, t):
                blk, d = divmod(t, D)
                wait(dve, tree, it, PAIR * ADDS, (t + 1) * ADDS)
                total, acc = leaves[:, t % SETS, 0, :], z2p[:, blk % 2, :]
                if d == 0:
                    wait(dve, m_turn, it, 2, blk - 1)
                    dve.tensor_scalar(acc, total, 0.0, None, ALU.max).then_inc(x2_set, 1)
                else:
                    wait(dve, x2_set, it, PAIR, t)
                    dve.scalar_tensor_tensor(out=acc, in0=total, scalar=0.0, in1=acc, op0=ALU.max,
                                             op1=ALU.add).then_inc(x2_set, 1)

            def body(it, first, last):
                for t in range(PAIR):
                    u, d = divmod(t, D)
                    r = t % SETS
                    for n in range(NB):
                        if DVE_BLOCKS[n]:
                            wait(dve, bank_full, it, PAIRB, t * NB + n + 1)
                        for k in range(DVE_BLOCKS[n]):
                            f = (DVE_UPTO[n - 1] if n else 0) + k
                            m = n * BANK + k
                            own = leaves[:, r, LEAVES - 2 + f % 2, :]
                            start = own
                            if f == 0:
                                start = b2r[:, :]
                            elif f == 1:
                                wait(dve, scaled, it, PAIR * NA, t * NA + 1)
                            else:
                                wait(dve, fma, it, PAIR * NF, t * NF + f - 1)
                            dve.scalar_tensor_tensor(out=own, in0=ps[:, n % RING, k * S:(k + 1) * S],
                                                     scalar=x0[:, u, d, m:m + 1], in1=start,
                                                     op0=ALU.mult, op1=ALU.add).then_inc(fma, 1)
                        s = (t % QUAD) * NB + n
                        q = t // QUAD + 1
                        if n == 5 and not (first and t < LAG):
                            finish(it, t - LAG)
                        if s == 36 and not (last and q + 1 >= QUADS):
                            low_x0(it, q + 1)
                        if (q % 4, s) == (1, 29) and not (first and u == 0):
                            copy_z2t(it, u - 1)
                        if last and q == QUADS:
                            continue
                        if s in range(5, 5 + 3 * KT, 3):
                            multiply(it, q, (s - 5) // 3)
                        if s == 31:
                            split_x1(it, q)
                        if s == 34:
                            sum_x1(it, q)
                if last:
                    for t in range(PAIR - LAG, PAIR):
                        finish(it, t)

            def copy_z2t(it, blk):
                wait(dve, m_turn, it, 2, blk + 1)
                dve.tensor_copy(z2t[:, :], ps[:, TR + z2_bank(blk), 0:P]).then_inc(m_z2t, 1)

            dve.memset(w1t[0:KR, 0, :], 0.0).then_inc(w1_zero, 1)
            dve.memset(xs[:, :].bitcast(F32), 0.0).then_inc(xs_zero, 1)
            dve.wait_ge(w1_in, 48)
            dve.tensor_tensor(w1c[0:KR, :, :], w1c[0:KR, :, :], w1t[0:KR, :, :], ALU.add).then_inc(w1_sum, 1)
            dve.wait_ge(w2_high, 1)
            dve.tensor_tensor(w2l[:, :], w2f, w2h[:, :].bitcast(F32), ALU.subtract).then_inc(w2_low, 1)
            dve.wait_ge(b_in, 32)
            low_x0(0, 0)
            for t in range(KT):
                multiply(0, 0, t)
            low_x0(0, 1)
            split_x1(0, 0)
            sum_x1(0, 0)
            iterations(dve, body)
            copy_z2t(ITERS - 1, 1)

        @block.tensor
        def _(pe):
            def turn(it, q):
                blk, quad = divmod(q, 4)
                wait(pe, x0_set, it, 2, blk + 1)
                wait(pe, pair_set, it, QUADS * KT, q * KT - 1)
                for i in range(QUAD):
                    mm = pe.transpose(ps[0:TURNED, TR + q * USES % 2, i * P:(i + 1) * P], x0[:, blk % 2, quad * QUAD + i, :],
                                      ident[:, :])
                mm.then_inc(turned, 1)

            def select(it, q, g):
                rows = KR if g < KT else (SHIFTS - PER * (KT - 1)) * M
                if g == 0:
                    wait(pe, lo0_set, it, QUADS, q + 1)
                    wait(pe, pair_set, it, QUADS * KT, q * KT)
                    if q % 4 == 2:
                        wait(pe, m_z2t, it, 2, q // 4)
                elif g == 2:
                    wait(pe, fac_set, it, QUADS, q + 1)
                elif g > 2:
                    wait(pe, pair_set, it, QUADS * KT, q * KT + g - 2)
                pe.matmul(ps[0:rows, TR + (q * USES + 1 + g) % 2, :], sels[:, g * KR:g * KR + rows], xs[:, :], start=True,
                          stop=True).then_inc(turned, 1)

            def contract(it, q, t):
                rows = KR if t < KT - 1 else (SHIFTS - PER * (KT - 1)) * M
                wait(pe, pair_set, it, QUADS * KT, q * KT + t + 1)
                if t == 0:
                    wait(pe, x1_set, it, QUADS, q)
                    if q % 4 == 2:
                        wait(pe, m_yc, it, 2, q // 4)
                mm = pe.matmul(ps[:, X1, :], w1c[0:rows, t, :], pair[0:rows, t, :], start=(t == 0), stop=(t == KT - 1))
                if t == KT - 1:
                    mm.then_inc(x1_sum, 1)

            def turn_z2(it, blk):
                wait(pe, x2_set, it, PAIR, (blk + 1) * D)
                wait(pe, pair_set, it, QUADS * KT, min(blk * 4 + 6, QUADS) * KT)
                pe.transpose(ps[:, TR + z2_bank(blk), 0:P], z2p[:, blk % 2, :], ident[:, :]).then_inc(m_turn, 1)

            def layer1(it, blk):
                u = blk % 2
                wait(pe, m_z2t, it, 2, blk + 1)
                wait(pe, z1_set, it, 2, blk + 1)
                wait(pe, x1_set, it, QUADS, min(blk * 4 + 6, QUADS))
                wait(pe, dense_in[u], it, 16, 16 * (blk // 2 + 1))
                zin = [(wt1s[:, 0, :], z1q[:, u, 0, :]), (wt1s[:, 1, :], z2t[:, :]), (wt1s[0:DN, 2, :], dts[:, u, :])]
                for m in range(N1):
                    for k, (w, x) in enumerate(zin):
                        mm = pe.matmul(ps[:, X1, m * P:(m + 1) * P], w[:, m * P:(m + 1) * P], x, start=(k == 0), stop=(k == 2))
                mm.then_inc(m_h1, 1)

            def layer2(it, blk):
                wait(pe, m_r1, it, 2 * N1, (blk + 1) * N1)
                for m in range(N2):
                    for k in range(N1):
                        mm = pe.matmul(ps[:, X1, m * P:(m + 1) * P], wt2s[:, k, m * P:(m + 1) * P], h1[:, k, :],
                                       start=(k == 0), stop=(k == N1 - 1))
                mm.then_inc(m_h2, 1)

            def layer3(it, blk):
                wait(pe, m_r2, it, 2 * N2, (blk + 1) * N2)
                for k in range(N2):
                    mm = pe.matmul(ps[0:1, X1, 0:P], wt3s[:, k:k + 1], h2[:, k, :], start=(k == 0), stop=(k == N2 - 1))
                mm.then_inc(m_y, 1)

            def body(it, first, last):
                for t in range(PAIR):
                    u = t // D
                    for n in range(NB):
                        s = (t % QUAD) * NB + n
                        q = t // QUAD + 1
                        if s == 32 and not (last and q + 1 >= QUADS):
                            turn(it, q + 1)
                        if not (first and u == 0):
                            if (q % 4, s) == (1, 28):
                                turn_z2(it, u - 1)
                            if (q % 4, s) == (1, 35):
                                layer1(it, u - 1)
                            if (q % 4, s) == (2, 1):
                                layer2(it, u - 1)
                            if (q % 4, s) == (2, 6):
                                layer3(it, u - 1)
                        if not (last and q == QUADS):
                            if s in range(1, 1 + 3 * (KT + 1), 3):
                                select(it, q, (s - 1) // 3)
                            if s in range(10, 10 + 3 * KT, 3):
                                contract(it, q, (s - 10) // 3)
                        if s == 0:
                            wait(pe, low_set, it, QUADS, q)
                            wait(pe, high_set, it, QUADS, q)
                        g = t * NB + n - RING
                        tt, nn = divmod(g, NB)
                        if nn in ACT_BANKS:
                            wait(pe, scaled, it, PAIR * NA, tt * NA + ACT_UPTO[nn])
                        else:
                            wait(pe, fma, it, PAIR * NF, tt * NF + DVE_UPTO[nn])
                        par, at = (t // QUAD) % 2, (t % QUAD) * P
                        hi, lo = x1h[:, par, at:at + P], x1l[:, par, at:at + P]
                        w = slice(n * BANK * S, (n * BANK + BLOCKS[n]) * S)
                        dst = ps[:, n % RING, 0:BLOCKS[n] * S]
                        pe.matmul(dst, hi, w2h[:, w], start=True, stop=False)
                        pe.matmul(dst, hi, w2l[:, w], start=False, stop=False)
                        pe.matmul(dst, lo, w2h[:, w], start=False, stop=True).then_inc(bank_full, 1)

            pe.wait_ge(set_up, 2)
            pe.wait_ge(w1_sum, 1)
            pe.wait_ge(sel_set, 1)
            turn(0, 0)
            for g in range(KT + 1):
                select(0, 0, g)
                if g > 1:
                    contract(0, 0, g - 2)
            contract(0, 0, KT - 1)
            turn(0, 1)
            pe.wait_ge(w2_low, 1)
            pe.wait_ge(mlp_in, 16 * MLP_LOADS)
            iterations(pe, body)
            turn_z2(ITERS - 1, 1)
            layer1(ITERS - 1, 1)
            layer2(ITERS - 1, 1)
            layer3(ITERS - 1, 1)


def kernel(**inputs):
    import numpy as np
    import concourse.bacc as bacc
    from concourse.bass_utils import run_bass_kernel_spmd

    a = {k: np.asarray(v) for k, v in inputs.items()}
    i = np.tile(np.arange(M), PER)[:, None]
    k = (np.arange(KR) // M)[:, None] + PER * np.arange(KT)[None, :]
    j = (i + k) % M
    row = np.arange(XR)[:, None, None] % LOW
    kk = np.concatenate([np.zeros((KR, 1), int), k], axis=1).T
    sel = (row == kk[None] + i[:, 0]) * np.ones(1, np.float32)
    w1 = a["L0_rec_W1"].transpose(1, 2, 0)
    arrays = {f"tbl_{f}": a[f"tbl_{f}"] for f in range(M)}
    arrays |= {
        "ids": a["ids"], "dense_t": a["dense_ctx"].T, "sel": sel.reshape(XR, -1),
        "w1a": w1[i, j], "w1b": w1[j, i], "b1": a["L0_rec_b1"],
        "w2": a["L0_rec_W2"].transpose(1, 2, 0).reshape(S, M * S), "b2": a["L0_rec_b2"],
        "wt1": a["W_top1"], "bt1": a["b_top1"].reshape(-1, P).T, "wt2": a["W_top2"],
        "bt2": a["b_top2"].reshape(-1, P).T, "wt3": a["W_top3"].reshape(-1, P).T,
    }
    arrays = {n: np.ascontiguousarray(x) for n, x in arrays.items()}
    nc = bacc.Bacc("TRN2", target_bir_lowering=False, num_devices=1)
    ap = {n: nc.dram_tensor(n, x.shape, mybir.dt.from_np(x.dtype), kind="ExternalInput").ap() for n, x in arrays.items()}
    out = nc.dram_tensor("y", (a["ids"].shape[0], 1), F32, kind="ExternalOutput").ap()
    tables = [ap[f"tbl_{f}"] for f in range(M)]
    cin_kernel(nc, tables, *(ap[n] for n in ("ids", "dense_t", "sel", "w1a", "w1b", "b1", "w2", "b2", "wt1", "bt1", "wt2",
                                             "bt2", "wt3")), out)
    r = run_bass_kernel_spmd(nc, [arrays], core_ids=[0])
    return r.results[0]["y"]
```

```python
from contextlib import ExitStack

import concourse.bass as bass
from concourse import mybir

F32 = mybir.dt.float32
F32R = mybir.dt.float32r
I32 = mybir.dt.int32
ALU = mybir.AluOpType
ACT = mybir.ActivationFunctionType
AX = mybir.AxisListType

P = 128
M = 39
D = 16
S = 128
PER = P // M
KR = PER * M
SHIFT = [(0, 0, 0), (1, 4, 6), (3, 15, 14), (10, 20, 27), (0, 17)]
EDGES = [(0, 1), (0, 2), (1, 2), (0, 3), (1, 3), (2, 3), (0, 4)]
KT = len(EDGES)
USES = len(SHIFT)
KEPT = USES - 1
ROWS = [M * len(SHIFT[g]) for _, g in EDGES]
LOW = 64
XR = LOW + M
COUNTED = sorted(min((b - a) % M, (a - b) % M) for f, g in EDGES for a, b in zip(SHIFT[f], SHIFT[g]))
assert COUNTED == list(range((M + 1) // 2)), "every pair of fields once"
QUAD = 4
BANK = 4
NB = -(-M // BANK)
RING = 5
SLOTS = QUAD * NB

ACT_BANKS = (0, 3, 5, 7)
BLOCKS = [min(BANK, M - BANK * n) for n in range(NB)]
ACT_BLOCKS = [BLOCKS[n] if n in ACT_BANKS else 0 for n in range(NB)]
DVE_BLOCKS = [0 if n in ACT_BANKS else BLOCKS[n] for n in range(NB)]
NA = sum(ACT_BLOCKS)
NF = sum(DVE_BLOCKS)
ACT_UPTO = [sum(ACT_BLOCKS[:n + 1]) for n in range(NB)]
DVE_UPTO = [sum(DVE_BLOCKS[:n + 1]) for n in range(NB)]
LEAVES = NA + 1
ADDS = 5
SETS = 4
LAG = 2

PAIR = 2 * D
QUADS = PAIR // QUAD
PAIRB = PAIR * NB
EARLY = 8
SELECT = [1, 5, 12, 24]
MULTIPLY = [3 + 4 * t for t in range(KT)]
CONTRACT = [8 + 4 * t for t in range(KT)]
TURN, PLAIN, LOW0 = 28, 30, 31
RELU_X1, SPLIT_X1 = 33, 35
SUM_X1, SUM_X2 = 9, 17
TURN_Z2, COPY_Z2, LAYER1, RELU_H1 = 32, 32, 38, 38
LAYER2, RELU_H2, LAYER3, COPY_Y = 1, 1, 4, 4
ARRANGE = 10
AHEAD = 15
GATHERS = [(M - AHEAD) * d // EARLY for d in range(EARLY + 1)]
GATHERS += [M - AHEAD + AHEAD * (d - EARLY) // (D - EARLY) for d in range(EARLY + 1, D + 1)]


def cin_kernel(nc, tables, ids, dense_t, sel, w1a, w1b, b1, w2, b2, wt1, bt1, wt2, bt2, wt3, out):
    B = ids.shape[0]
    NBLK = B // P
    ITERS = NBLK // 2
    DN = dense_t.shape[0]
    N1 = wt1.shape[1] // P
    N2 = wt2.shape[1] // P

    with ExitStack() as ctx:
        def sb(name, shape, dt=F32):
            return ctx.enter_context(nc.sbuf_tensor(name, shape, dt))

        def sem(name):
            return ctx.enter_context(nc.semaphore(name))

        w2h = sb("w2h", [P, M * S], F32R)
        w2l = sb("w2l", [P, M * S], F32R)
        leaves = sb("leaves", [P, SETS, LEAVES, S])
        leaves_flat = leaves[:].rearrange("p a b c -> p (a b c)")
        w2f = leaves_flat[:, 0:M * S]
        w1c = sb("w1c", [P, KT, S])
        w1t = sb("w1t", [P, KT, S])
        ident = sb("ident", [P, P])
        b1c = sb("b1c", [P, 1])
        b2r = sb("b2r", [P, S])
        idx = sb("idx", [P, 2, M], I32)
        emb = sb("emb", [P, 2, M * D])
        x0 = sb("x0", [P, 2, D, KR])
        xs = sb("xs", [XR, QUAD * P], F32R)
        sels = sb("sels", [XR, KEPT * KR], F32R)
        sels_f32 = sb("sels_f32", [XR, KEPT * KR])
        fac = sb("fac", [P, KEPT, QUAD * P])
        pair = sb("pair", [P, KT, QUAD * P])
        x1f = sb("x1f", [P, 2, QUAD * P])
        x1h = sb("x1h", [P, 2, QUAD * P], F32R)
        x1l = sb("x1l", [P, 2, QUAD * P], F32R)
        z1q = sb("z1q", [P, 2, QUAD, P])
        x2r = sb("x2r", [P, 2, QUAD, S])
        z2q = sb("z2q", [P, 2, QUAD, S])
        wt1s = sb("wt1s", [P, 3, N1 * P])
        wt2s = sb("wt2s", [P, N1, N2 * P])
        wt3s = sb("wt3s", [P, N2])
        bt1s = sb("bt1s", [P, N1])
        bt2s = sb("bt2s", [P, N2])
        dts = sb("dts", [DN, 2, P])
        z2t = sb("z2t", [S, P])
        h1 = sb("h1", [P, N1, P])
        h2 = sb("h2", [P, N2, P])
        yrow = sb("yrow", [1, 2, P])

        ps = ctx.enter_context(nc.psum_tensor("ps", [P, 8, 512], F32))
        TR, X1 = RING, RING + 2

        w1_in = sem("w1_in")
        b_in = sem("b_in")
        mlp_in = sem("mlp_in")
        w2_in = sem("w2_in")
        ident_set = sem("ident_set")
        w1_zero = sem("w1_zero")
        xs_zero = sem("xs_zero")
        w1_sum = sem("w1_sum")
        w2_high = sem("w2_high")
        w2_low = sem("w2_low")
        idx_in = [sem("idx_in0"), sem("idx_in1")]
        gathered = [sem("gathered0"), sem("gathered1")]
        x0_set = sem("x0_set")
        sel_in = sem("sel_in")
        sel_set = sem("sel_set")
        dense_in = [sem("dense_in0"), sem("dense_in1")]
        hi0_set = sem("hi0_set")
        lo0_set = sem("lo0_set")
        turned = sem("turned")
        fac_set = sem("fac_set")
        pair_set = sem("pair_set")
        x1_sum = sem("x1_sum")
        x1_set = sem("x1_set")
        high_set = sem("high_set")
        low_set = sem("low_set")
        z1q_set = sem("z1q_set")
        z1_half = sem("z1_half")
        z1_set = sem("z1_set")
        bank_full = sem("bank_full")
        fma = sem("fma")
        scaled = sem("scaled")
        tree = sem("tree")
        x2_set = sem("x2_set")
        z2q_set = sem("z2q_set")
        z2_half = sem("z2_half")
        z2_set = sem("z2_set")
        m_turn = sem("m_turn")
        m_z2t = sem("m_z2t")
        m_h1 = sem("m_h1")
        m_r1 = sem("m_r1")
        m_h2 = sem("m_h2")
        m_r2 = sem("m_r2")
        m_y = sem("m_y")
        m_yc = sem("m_yc")
        y_out = [sem("y_out0"), sem("y_out1")]
        MLP_LOADS = 6

        block = ctx.enter_context(nc.Block())

        def wait(eng, s, it, per, k):
            v = it * per + k
            if isinstance(v, int) and v <= 0:
                return
            eng.wait_ge(s, v)

        def iterations(eng, body):
            body(0, True, False)
            with eng.Fori(1, ITERS - 1) as it:
                body(it, False, False)
            body(ITERS - 1, False, True)

        out_rows = out.rearrange("(k b) a -> k (b a)", b=P)

        @block.sync
        def _(sp):
            for u in range(2):
                sp.dma_start(idx[:, u, :], ids[u * P:(u + 1) * P, :]).then_inc(idx_in[u], 16)
            sp.dma_start(sels_f32[:, :], sel).then_inc(sel_in, 16)
            for u in range(2):
                sp.dma_start(dts[:, u, :], dense_t[:, u * P:(u + 1) * P]).then_inc(dense_in[u], 16)
            sp.dma_start(w1c[0:KR, :, :], w1a).then_inc(w1_in, 16)
            sp.wait_ge(w1_zero, 1)
            sp.dma_start(w1t[M:ROWS[-1], KT - 1, :], w1b[M:ROWS[-1], KT - 1, :]).then_inc(w1_in, 16)
            sp.dma_start(w1t[0:KR, 0:KT - 1, :], w1b[:, 0:KT - 1, :]).then_inc(w1_in, 16)
            sp.dma_start(b1c[:, :], b1.rearrange("(p a) -> p a", a=1)).then_inc(b_in, 16)
            sp.dma_start(w2f, w2).then_inc(w2_in, 16)
            sp.dma_start(b2r[:, :], b2.rearrange("(a s) -> a s", a=1).broadcast_to([P, S])).then_inc(b_in, 16)
            sp.dma_start(wt1s[:, 0:2, :], wt1[0:2 * P, :].rearrange("(k p) n -> p k n", p=P)).then_inc(mlp_in, 16)
            sp.dma_start(wt1s[0:DN, 2, :], wt1[2 * P:2 * P + DN, :]).then_inc(mlp_in, 16)
            sp.dma_start(wt2s[:, :, :], wt2.rearrange("(k p) n -> p k n", p=P)).then_inc(mlp_in, 16)
            sp.dma_start(wt3s[:, :], wt3).then_inc(mlp_in, 16)
            sp.dma_start(bt1s[:, :], bt1).then_inc(mlp_in, 16)
            sp.dma_start(bt2s[:, :], bt2).then_inc(mlp_in, 16)

            def body(it, first, last):
                for u in range(2):
                    if not first or u == 1:
                        blk = u - 1
                        v = blk % 2
                        wait(sp, m_yc, it, 2, blk + 1)
                        sp.dma_start(out_rows[bass.ds(it * 2 + blk, 1), :], yrow[0:1, v, :]).then_inc(y_out[v], 16)
                        if not (last and u == 1):
                            sp.dma_start(dts[:, v, :], dense_t[:, bass.ds((it * 2 + blk + 2) * P, P)]).then_inc(dense_in[v], 16)
                    if not last:
                        wait(sp, gathered[u], it, 16 * M, 16 * M)
                        sp.dma_start(idx[:, u, :], ids[bass.ds((it * 2 + u + 2) * P, P), :]).then_inc(idx_in[u], 16)

            iterations(sp, body)
            sp.wait_ge(m_yc, NBLK)
            sp.dma_start(out_rows[NBLK - 1:NBLK, :], yrow[0:1, 1, :]).then_inc(y_out[1], 16)
            for u in range(2):
                sp.wait_ge(y_out[u], 16 * ITERS)

        @block.gpsimd
        def _(pool):
            pool.memset(ident[:, :], 0.0).then_inc(ident_set, 1)
            pool.wait_ge(ident_set, 1)
            pool.affine_select(out=ident[:, :], in_=ident[:, :], compare_op=ALU.not_equal, fill=1.0, base=0,
                               pattern=[[-1, P]], channel_multiplier=1).then_inc(ident_set, 1)

            def gather(u, f0, f1):
                for f in range(f0, f1):
                    pool.indirect_dma_start(
                        out=emb[:, u, f * D:(f + 1) * D], out_offset=None, in_=tables[f],
                        in_offset=bass.IndirectOffsetOnAxis(ap=idx[:, u, f:f + 1], axis=0)).then_inc(gathered[u], 16)

            def add_quads(it, blk, quads, quads_set, half, whole):
                u = blk % 2
                wait(pool, quads_set, it, QUADS, (blk + 1) * 4)
                pool.tensor_tensor(quads[:, u, 0:2, :], quads[:, u, 0:2, :], quads[:, u, 2:4, :], ALU.add).then_inc(half, 1)
                wait(pool, half, it, 2, blk + 1)
                pool.tensor_tensor(quads[:, u, 0, :], quads[:, u, 0, :], quads[:, u, 1, :], ALU.add).then_inc(whole, 1)

            def body(it, first, last):
                for t in range(PAIR):
                    u, d = divmod(t, D)
                    ahead = 1 if d < EARLY else 2
                    blk = u + ahead
                    v = blk % 2
                    if not (last and blk > 1):
                        if d == EARLY:
                            wait(pool, idx_in[v], it, 16, 16 * (blk // 2 + 1))
                            wait(pool, x0_set, it, 2 * PER, (blk - 1) * PER)
                    if d == D - 2:
                        add_quads(it, u, z1q, z1q_set, z1_half, z1_set)
                    if d == 3 and not (first and u == 0):
                        add_quads(it, u - 1, z2q, z2q_set, z2_half, z2_set)
                    r = t % SETS
                    wait(pool, scaled, it, PAIR * NA, (t + 1) * NA)
                    wait(pool, fma, it, PAIR * NF, (t + 1) * NF)
                    steps = [(leaves[:, r, 0:8, :], leaves[:, r, 8:16, :]),
                             (leaves[:, r, 0:4, :], leaves[:, r, 4:8, :]),
                             (leaves[:, r, 0:2, :], leaves[:, r, 2:4, :]),
                             (leaves[:, r, 0, :], leaves[:, r, 1, :]),
                             (leaves[:, r, 0, :], leaves[:, r, 16, :])]
                    for k, (a, b) in enumerate(steps):
                        if k:
                            wait(pool, tree, it, PAIR * ADDS, t * ADDS + k)
                        pool.tensor_tensor(a, a, b, ALU.add).then_inc(tree, 1)
                    if not (last and blk > 1):
                        done = M - AHEAD if ahead == 2 else -AHEAD
                        gather(v, GATHERS[d] - done, GATHERS[d + 1] - done)

            pool.wait_ge(idx_in[0], 16)
            gather(0, 0, M)
            pool.wait_ge(idx_in[1], 16)
            gather(1, 0, AHEAD)
            iterations(pool, body)
            add_quads(ITERS - 1, 1, z2q, z2q_set, z2_half, z2_set)

        @block.scalar
        def _(act):
            def arrange(it, u, blk, j):
                wait(act, gathered[u], it, 16 * M, 16 * M * (blk // 2 + 1))
                wait(act, fma, it, PAIR * NF, (blk - 1) * D * NF)
                act.copy(x0[:, u, :, j * M:(j + 1) * M], emb[:, u, :].rearrange("p (f d) -> p d f", d=D)).then_inc(x0_set, 1)

            def plain_x0(it, q):
                wait(act, turned, it, QUADS * USES, q * USES + 1)
                act.copy(xs[0:M, :], ps[0:M, TR + q % 2, :]).then_inc(hi0_set, 1)
                wait(act, pair_set, it, QUADS * KT, q * KT)
                act.copy(fac[0:KR, 0, :], ps[0:KR, TR + q % 2, :]).then_inc(fac_set, 1)

            def keep_factor(it, q, g):
                wait(act, turned, it, QUADS * USES, q * USES + g + 1)
                act.copy(fac[0:KR, g, :], ps[0:KR, TR + (q + g) % 2, :]).then_inc(fac_set, 1)

            def relu_x1(it, q):
                wait(act, x1_sum, it, QUADS, q + 1)
                wait(act, z1q_set, it, QUADS, q - 1)
                act.activation(x1f[:, q % 2, :], ps[:, X1, :], ACT.Relu, bias=b1c[:, :]).then_inc(x1_set, 1)
                wait(act, x1_set, it, QUADS, q + 1)
                wait(act, bank_full, it, PAIRB, (q - 1) * SLOTS)
                act.copy(x1h[:, q % 2, :], x1f[:, q % 2, :]).then_inc(high_set, 1)

            def relu_x2(it, t):
                quad = t // QUAD
                wait(act, tree, it, PAIR * ADDS, (t + 1) * ADDS)
                wait(act, z2q_set, it, QUADS, quad - 1)
                act.activation(x2r[:, quad % 2, t % QUAD, :], leaves[:, t % SETS, 0, :], ACT.Relu).then_inc(x2_set, 1)

            def relu_h1(it, blk):
                wait(act, m_h1, it, 2, blk + 1)
                for m in range(N1):
                    act.activation(h1[:, m, :], ps[:, X1, m * P:(m + 1) * P], ACT.Relu, bias=bt1s[:, m:m + 1]).then_inc(m_r1, 1)

            def relu_h2(it, blk):
                wait(act, m_h2, it, 2, blk + 1)
                for m in range(N2):
                    act.activation(h2[:, m, :], ps[:, X1, m * P:(m + 1) * P], ACT.Relu, bias=bt2s[:, m:m + 1]).then_inc(m_r2, 1)

            def copy_y(it, blk):
                wait(act, m_y, it, 2, blk + 1)
                wait(act, y_out[blk % 2], it, 16, 16 * (blk // 2))
                act.copy(yrow[0:1, blk % 2, :], ps[0:1, X1, 0:P]).then_inc(m_yc, 1)

            def body(it, first, last):
                for t in range(PAIR):
                    u, d = divmod(t, D)
                    r = t % SETS
                    wait(act, x2_set, it, PAIR, t - SETS + 1)
                    for n in range(NB):
                        if ACT_BLOCKS[n]:
                            wait(act, bank_full, it, PAIRB, t * NB + n + 1)
                        for k in range(ACT_BLOCKS[n]):
                            a = (ACT_UPTO[n - 1] if n else 0) + k
                            m = n * BANK + k
                            slot = LEAVES - 1 if a == 0 else a - 1
                            act.activation(leaves[:, r, slot, :], ps[:, n % RING, k * S:(k + 1) * S], ACT.Copy,
                                           scale=x0[:, u, d, m:m + 1]).then_inc(scaled, 1)
                        s = (t % QUAD) * NB + n
                        q = t // QUAD + 1
                        if n == 5 and not (first and t < LAG):
                            relu_x2(it, t - LAG)
                        if d == ARRANGE and n in (0, 2, 4) and not (last and u == 1):
                            arrange(it, (u + 1) % 2, u + 1, n // 2)
                        if s == PLAIN and not (last and q + 1 >= QUADS):
                            plain_x0(it, q + 1)
                        if not (first and u == 0):
                            if (q % 4, s) == (2, RELU_H1):
                                relu_h1(it, u - 1)
                            if (q % 4, s) == (3, RELU_H2):
                                relu_h2(it, u - 1)
                            if (q % 4, s) == (3, COPY_Y):
                                copy_y(it, u - 1)
                        if last and q == QUADS:
                            continue
                        if s in SELECT[:KEPT - 1]:
                            keep_factor(it, q, SELECT.index(s) + 1)
                        if s == RELU_X1:
                            relu_x1(it, q)

            act.wait_ge(sel_in, 16)
            act.copy(sels[:, :], sels_f32[:, :]).then_inc(sel_set, 1)
            act.wait_ge(w2_in, 16)
            act.copy(w2h[:, :], w2f).then_inc(w2_high, 1)
            act.wait_ge(b_in, 32)
            act.wait_ge(xs_zero, 1)
            for j in range(PER):
                arrange(0, 0, 0, j)
            plain_x0(0, 0)
            for g in range(1, KEPT):
                keep_factor(0, 0, g)
            relu_x1(0, 0)
            plain_x0(0, 1)
            act.wait_ge(w2_low, 1)
            act.wait_ge(mlp_in, 16 * MLP_LOADS)
            iterations(act, body)
            for t in range(PAIR - LAG, PAIR):
                relu_x2(ITERS - 1, t)
            relu_h1(ITERS - 1, 1)
            relu_h2(ITERS - 1, 1)
            copy_y(ITERS - 1, 1)

        @block.vector
        def _(dve):
            def multiply(it, q, t):
                rows, (f, g) = ROWS[t], EDGES[t]
                if g < KEPT:
                    wait(dve, fac_set, it, QUADS * KEPT, q * KEPT + g + 1)
                else:
                    wait(dve, turned, it, QUADS * USES, q * USES + g + 1)
                if t == 0:
                    wait(dve, x1_sum, it, QUADS, q)
                dve.tensor_tensor(pair[0:rows, t, :], ps[0:rows, TR + (q + g) % 2, :], fac[0:rows, f, :],
                                  ALU.mult).then_inc(pair_set, 1)

            def low_x0(it, q):
                wait(dve, hi0_set, it, QUADS, q + 1)
                wait(dve, fac_set, it, QUADS * KEPT, q * KEPT + 1)
                dve.tensor_tensor(xs[LOW:XR, :], ps[0:M, TR + q % 2, :], xs[0:M, :].bitcast(F32),
                                  ALU.subtract).then_inc(lo0_set, 1)

            def split_x1(it, q):
                blk, quad = divmod(q, 4)
                wait(dve, high_set, it, QUADS, q + 1)
                wait(dve, bank_full, it, PAIRB, (q - 1) * SLOTS)
                dve.tensor_tensor(x1l[:, q % 2, :], x1f[:, q % 2, :], x1h[:, q % 2, :].bitcast(F32),
                                  ALU.subtract).then_inc(low_set, 1)

            def sum_x1(it, q):
                blk, quad = divmod(q, 4)
                if quad == 0:
                    wait(dve, m_h1, it, 2, blk - 1)
                dve.tensor_reduce(z1q[:, blk % 2, quad, :], x1f[:, q % 2, :].rearrange("p (d b) -> p b d", d=QUAD),
                                  AX.X, ALU.add).then_inc(z1q_set, 1)

            def sum_x2(it, quad):
                blk = quad // 4
                wait(dve, x2_set, it, PAIR, (quad + 1) * QUAD)
                if quad % 4 == 0:
                    wait(dve, m_turn, it, 2, blk - 1)
                dve.tensor_reduce(z2q[:, blk % 2, quad % 4, :], x2r[:, quad % 2, :, :].rearrange("p d s -> p s d"),
                                  AX.X, ALU.add).then_inc(z2q_set, 1)

            def body(it, first, last):
                for t in range(PAIR):
                    u, d = divmod(t, D)
                    r = t % SETS
                    for n in range(NB):
                        if DVE_BLOCKS[n]:
                            wait(dve, bank_full, it, PAIRB, t * NB + n + 1)
                        for k in range(DVE_BLOCKS[n]):
                            f = (DVE_UPTO[n - 1] if n else 0) + k
                            m = n * BANK + k
                            own = leaves[:, r, LEAVES - 2 + f % 2, :]
                            start = own
                            if f == 0:
                                start = b2r[:, :]
                                wait(dve, tree, it, PAIR * ADDS, (t - SETS + 1) * ADDS)
                            elif f == 1:
                                wait(dve, scaled, it, PAIR * NA, t * NA + 1)
                            else:
                                wait(dve, fma, it, PAIR * NF, t * NF + f - 1)
                            dve.scalar_tensor_tensor(out=own, in0=ps[:, n % RING, k * S:(k + 1) * S],
                                                     scalar=x0[:, u, d, m:m + 1], in1=start,
                                                     op0=ALU.mult, op1=ALU.add).then_inc(fma, 1)
                        s = (t % QUAD) * NB + n
                        q = t // QUAD + 1
                        if s == SUM_X1:
                            sum_x1(it, q - 1)
                        if s == SUM_X2 and not (first and q == 1):
                            sum_x2(it, q - 2)
                        if s == LOW0 and not (last and q + 1 >= QUADS):
                            low_x0(it, q + 1)
                        if (q % 4, s) == (2, COPY_Z2) and not (first and u == 0):
                            copy_z2t(it, u - 1)
                        if last and q == QUADS:
                            continue
                        if s in MULTIPLY:
                            multiply(it, q, MULTIPLY.index(s))
                        if s == SPLIT_X1:
                            split_x1(it, q)

            def copy_z2t(it, blk):
                wait(dve, m_turn, it, 2, blk + 1)
                dve.tensor_copy(z2t[:, :], ps[:, TR, 0:P]).then_inc(m_z2t, 1)

            dve.memset(w1t[0:KR, KT - 1, :], 0.0).then_inc(w1_zero, 1)
            dve.memset(xs[:, :].bitcast(F32), 0.0).then_inc(xs_zero, 1)
            dve.wait_ge(w1_in, 48)
            dve.tensor_tensor(w1c[0:KR, :, :], w1c[0:KR, :, :], w1t[0:KR, :, :], ALU.add).then_inc(w1_sum, 1)
            dve.wait_ge(w2_high, 1)
            dve.tensor_tensor(w2l[:, :], w2f, w2h[:, :].bitcast(F32), ALU.subtract).then_inc(w2_low, 1)
            dve.wait_ge(b_in, 32)
            low_x0(0, 0)
            for t in range(KT):
                multiply(0, 0, t)
            split_x1(0, 0)
            low_x0(0, 1)
            iterations(dve, body)
            sum_x2(ITERS - 1, QUADS - 1)
            copy_z2t(ITERS - 1, 1)

        @block.tensor
        def _(pe):
            def turn(it, q):
                blk, quad = divmod(q, 4)
                wait(pe, x0_set, it, 2 * PER, (blk + 1) * PER)
                wait(pe, pair_set, it, QUADS * KT, q * KT - 1)
                for i in range(QUAD):
                    mm = pe.transpose(ps[0:KR, TR + q % 2, i * P:(i + 1) * P], x0[:, blk % 2, quad * QUAD + i, :],
                                      ident[:, :])
                mm.then_inc(turned, 1)

            def select(it, q, g):
                rows = M * len(SHIFT[g])
                if g == 1:
                    wait(pe, lo0_set, it, QUADS, q + 1)
                    wait(pe, pair_set, it, QUADS * KT, q * KT)
                    if q % 4 == 3:
                        wait(pe, m_z2t, it, 2, q // 4)
                elif g > 2:
                    wait(pe, pair_set, it, QUADS * KT, q * KT + 1 + max(t for t in range(KT) if EDGES[t][1] == g - 2))
                pe.matmul(ps[0:rows, TR + (q + g) % 2, :], sels[:, (g - 1) * KR:(g - 1) * KR + rows], xs[:, :], start=True,
                          stop=True).then_inc(turned, 1)

            def contract(it, q, t):
                rows = ROWS[t]
                wait(pe, pair_set, it, QUADS * KT, q * KT + t + 1)
                if t == 0:
                    wait(pe, x1_set, it, QUADS, q)
                    if q % 4 == 3:
                        wait(pe, m_yc, it, 2, q // 4)
                mm = pe.matmul(ps[:, X1, :], w1c[0:rows, t, :], pair[0:rows, t, :], start=(t == 0), stop=(t == KT - 1))
                if t == KT - 1:
                    mm.then_inc(x1_sum, 1)

            def turn_z2(it, blk):
                wait(pe, z2_set, it, 2, blk + 1)
                wait(pe, pair_set, it, QUADS * KT, min(blk * 4 + 7, QUADS) * KT)
                pe.transpose(ps[:, TR, 0:P], z2q[:, blk % 2, 0, :], ident[:, :]).then_inc(m_turn, 1)

            def layer1(it, blk):
                u = blk % 2
                wait(pe, m_z2t, it, 2, blk + 1)
                wait(pe, z1_set, it, 2, blk + 1)
                wait(pe, x1_set, it, QUADS, min(blk * 4 + 7, QUADS))
                wait(pe, dense_in[u], it, 16, 16 * (blk // 2 + 1))
                zin = [(wt1s[:, 0, :], z1q[:, u, 0, :]), (wt1s[:, 1, :], z2t[:, :]), (wt1s[0:DN, 2, :], dts[:, u, :])]
                for m in range(N1):
                    for k, (w, x) in enumerate(zin):
                        mm = pe.matmul(ps[:, X1, m * P:(m + 1) * P], w[:, m * P:(m + 1) * P], x, start=(k == 0), stop=(k == 2))
                mm.then_inc(m_h1, 1)

            def layer2(it, blk):
                wait(pe, m_r1, it, 2 * N1, (blk + 1) * N1)
                for m in range(N2):
                    for k in range(N1):
                        mm = pe.matmul(ps[:, X1, m * P:(m + 1) * P], wt2s[:, k, m * P:(m + 1) * P], h1[:, k, :],
                                       start=(k == 0), stop=(k == N1 - 1))
                mm.then_inc(m_h2, 1)

            def layer3(it, blk):
                wait(pe, m_r2, it, 2 * N2, (blk + 1) * N2)
                for k in range(N2):
                    mm = pe.matmul(ps[0:1, X1, 0:P], wt3s[:, k:k + 1], h2[:, k, :], start=(k == 0), stop=(k == N2 - 1))
                mm.then_inc(m_y, 1)

            def body(it, first, last):
                for t in range(PAIR):
                    u = t // D
                    for n in range(NB):
                        s = (t % QUAD) * NB + n
                        q = t // QUAD + 1
                        if s == TURN and not (last and q + 1 >= QUADS):
                            turn(it, q + 1)
                        if not (first and u == 0):
                            if (q % 4, s) == (2, TURN_Z2):
                                turn_z2(it, u - 1)
                            if (q % 4, s) == (2, LAYER1):
                                layer1(it, u - 1)
                            if (q % 4, s) == (3, LAYER2):
                                layer2(it, u - 1)
                            if (q % 4, s) == (3, LAYER3):
                                layer3(it, u - 1)
                        if not (last and q == QUADS):
                            if s in SELECT:
                                select(it, q, SELECT.index(s) + 1)
                            if s in CONTRACT:
                                contract(it, q, CONTRACT.index(s))
                        if s == 0:
                            wait(pe, low_set, it, QUADS, q)
                            wait(pe, high_set, it, QUADS, q)
                        g = t * NB + n - RING
                        tt, nn = divmod(g, NB)
                        if nn in ACT_BANKS:
                            wait(pe, scaled, it, PAIR * NA, tt * NA + ACT_UPTO[nn])
                        else:
                            wait(pe, fma, it, PAIR * NF, tt * NF + DVE_UPTO[nn])
                        par, at = (t // QUAD) % 2, (t % QUAD) * P
                        hi, lo = x1h[:, par, at:at + P], x1l[:, par, at:at + P]
                        w = slice(n * BANK * S, (n * BANK + BLOCKS[n]) * S)
                        dst = ps[:, n % RING, 0:BLOCKS[n] * S]
                        pe.matmul(dst, hi, w2h[:, w], start=True, stop=False)
                        pe.matmul(dst, hi, w2l[:, w], start=False, stop=False)
                        pe.matmul(dst, lo, w2h[:, w], start=False, stop=True).then_inc(bank_full, 1)

            pe.wait_ge(ident_set, 2)
            pe.wait_ge(w1_sum, 1)
            pe.wait_ge(sel_set, 1)
            turn(0, 0)
            select(0, 0, 1)
            select(0, 0, 2)
            for t in range(KT):
                contract(0, 0, t)
                if t == 0 or t == 2:
                    select(0, 0, 3 + t // 2)
            turn(0, 1)
            pe.wait_ge(w2_low, 1)
            pe.wait_ge(mlp_in, 16 * MLP_LOADS)
            iterations(pe, body)
            turn_z2(ITERS - 1, 1)
            layer1(ITERS - 1, 1)
            layer2(ITERS - 1, 1)
            layer3(ITERS - 1, 1)


def kernel(**inputs):
    import numpy as np
    import concourse.bacc as bacc
    from concourse.bass_utils import run_bass_kernel_spmd

    a = {k: np.asarray(v) for k, v in inputs.items()}
    field = np.array([[(i + k) % M for k in (*SHIFT[g], 0)[:PER] for i in range(M)] for g in range(USES)])
    i, j = (field[[e[n] for e in EDGES]].T for n in range(2))
    row = np.arange(XR)[:, None, None] % LOW
    sel = (row == field[None, 1:]) * np.ones(1, np.float32)
    w1 = a["L0_rec_W1"].transpose(1, 2, 0)
    arrays = {f"tbl_{f}": a[f"tbl_{f}"] for f in range(M)}
    arrays |= {
        "ids": a["ids"], "dense_t": a["dense_ctx"].T, "sel": sel.reshape(XR, -1),
        "w1a": w1[i, j], "w1b": w1[j, i], "b1": a["L0_rec_b1"],
        "w2": a["L0_rec_W2"].transpose(1, 2, 0).reshape(S, M * S), "b2": a["L0_rec_b2"],
        "wt1": a["W_top1"], "bt1": a["b_top1"].reshape(-1, P).T, "wt2": a["W_top2"],
        "bt2": a["b_top2"].reshape(-1, P).T, "wt3": a["W_top3"].reshape(-1, P).T,
    }
    arrays = {n: np.ascontiguousarray(x) for n, x in arrays.items()}
    nc = bacc.Bacc("TRN2", target_bir_lowering=False, num_devices=1)
    ap = {n: nc.dram_tensor(n, x.shape, mybir.dt.from_np(x.dtype), kind="ExternalInput").ap() for n, x in arrays.items()}
    out = nc.dram_tensor("y", (a["ids"].shape[0], 1), F32, kind="ExternalOutput").ap()
    tables = [ap[f"tbl_{f}"] for f in range(M)]
    cin_kernel(nc, tables, *(ap[n] for n in ("ids", "dense_t", "sel", "w1a", "w1b", "b1", "w2", "b2", "wt1", "bt1", "wt2",
                                             "bt2", "wt3")), out)
    r = run_bass_kernel_spmd(nc, [arrays], core_ids=[0])
    return r.results[0]["y"]
```
